# Optimizing a Trainium2 kernel written in Bass

```python
import numpy as np
import jax
import jax.numpy as jnp

def _softmax(x, axis=-1):
    return jax.nn.softmax(x, axis=axis)

def _gelu(x):
    return jax.nn.gelu(x, approximate=True)

def _silu(x):
    return jax.nn.silu(x)

def _sigmoid(x):
    return jax.nn.sigmoid(x)

def _layernorm(x, axis=-1, eps=1e-05):
    m = jnp.mean(x, axis=axis, keepdims=True)
    v = jnp.var(x, axis=axis, keepdims=True)
    return (x - m) / jnp.sqrt(v + eps)

def _scatter_add(tgt, idx, src, axis=0):
    return tgt.at[idx].add(src)

def _segment_sum(src, seg, n):
    return jax.ops.segment_sum(src, seg, n)
kernel_name = 'mk_gnn_resnorm_d2_gnn_r32_349ee1'

def setup_inputs(seed: int=0):
    np.random.seed(seed)
    _w = jnp.asarray

    def _rec_inputs():
        import jax
        import jax.numpy as jnp
        _gk = jax.random.key(seed)
        x = 0.0001712 + 1 * jax.random.normal(jax.random.fold_in(_gk, 1), (3125, 16), jnp.float32)
        _s = jax.random.randint(jax.random.fold_in(_gk, 2), (50000,), 0, 3125, jnp.int32)
        _d = jax.random.randint(jax.random.fold_in(_gk, 3), (50000,), 0, 3125, jnp.int32)
        _loop = jnp.arange(3125, dtype=jnp.int32)
        src = jnp.concatenate([_s, _d, _loop])
        dst = jnp.concatenate([_d, _s, _loop])
        _o = jnp.argsort(dst, stable=True)
        src = src[_o]
        dst = dst[_o]
        edge_attr_16 = 5.96457e-05 + 0.999887 * jax.random.normal(jax.random.fold_in(_gk, 11), (103125, 16), jnp.float32)
        return (x, src, dst, edge_attr_16)
    x, src, dst, edge_attr_16 = _rec_inputs()

    def _L0_gnn_setup():
        import jax, jax.numpy as jnp
        import numpy as np
        N_NODES = 50000
        N_EDGES = 25000
        D = 16
        key = jax.random.key(seed)
        k1, k2, k3, k4 = jax.random.split(key, 4)
        x = jax.random.normal(k1, (N_NODES, D), dtype=jnp.float32)
        edge_index = jax.random.randint(k2, (2, N_EDGES), 0, N_NODES, dtype=jnp.int64)
        W_tp = jax.random.normal(k3, (D, D, D), dtype=jnp.float32) * (1.0 / D)
        weight = jax.random.normal(k4, (D, D), dtype=jnp.float32) * 0.01
        bias = jnp.zeros((D,), dtype=jnp.float32)
        return {'x': x, 'edge_index': edge_index, 'W_tp': W_tp, 'weight': weight, 'bias': bias}
    _L0_gnn_all = _L0_gnn_setup()
    _L0_gnn_in = {k: v for k, v in _L0_gnn_all.items() if k in ('W_tp', 'weight', 'bias')}
    del _L0_gnn_all

    def _L1_gnn_setup():
        import jax, jax.numpy as jnp
        import numpy as np
        N_ATOMS = 625
        N_EDGES = 20000
        ATOM_DIM = 16
        BOND_DIM = 16
        key = jax.random.key(seed)
        k1, k2, k3, k4 = jax.random.split(key, 4)
        atom_features = jax.random.normal(k1, (N_ATOMS, ATOM_DIM), dtype=jnp.float32)
        bond_features = jax.random.normal(k2, (N_EDGES, BOND_DIM), dtype=jnp.float32)
        pair_indices = jax.random.randint(k3, (N_EDGES, 2), 0, N_ATOMS, dtype=jnp.int32)
        kernel = jax.random.normal(k4, (BOND_DIM, ATOM_DIM * ATOM_DIM), dtype=jnp.float32) * 0.05
        bias = jnp.zeros((ATOM_DIM * ATOM_DIM,), dtype=jnp.float32)
        return {'atom_features': atom_features, 'bond_features': bond_features, 'pair_indices': pair_indices, 'kernel': kernel, 'bias': bias}
    _L1_gnn_all = _L1_gnn_setup()
    _L1_gnn_in = {k: v for k, v in _L1_gnn_all.items() if k in ('kernel', 'bias')}
    del _L1_gnn_all
    return {'x': x, 'src': src, 'dst': dst, 'edge_attr_16': edge_attr_16, 'L0_gnn_W_tp': _L0_gnn_in['W_tp'], 'L0_gnn_weight': _L0_gnn_in['weight'], 'L0_gnn_bias': _L0_gnn_in['bias'], 'L1_gnn_kernel': _L1_gnn_in['kernel'], 'L1_gnn_bias': _L1_gnn_in['bias']}

def reference(x, src, dst, edge_attr_16, L0_gnn_W_tp, L0_gnn_weight, L0_gnn_bias, L1_gnn_kernel, L1_gnn_bias):
    import jax
    import jax.numpy as jnp

    def _L0_gnn_ref(x, edge_index, W_tp, weight, bias):
        import jax, jax.numpy as jnp
        import numpy as np
        N_NODES = 50000
        N_EDGES = 25000
        D = 16
        row, col = (edge_index[0], edge_index[1])
        xr = x[row]
        xc = x[col]
        messages = jnp.einsum('eu,ev,uvw->ew', xr, xc, W_tp)
        out = jnp.zeros((x.shape[0], D), dtype=x.dtype).at[row].add(messages)
        return out @ weight.T + bias

    def _L1_gnn_ref(atom_features, bond_features, pair_indices, kernel, bias):
        import jax, jax.numpy as jnp
        import numpy as np
        N_ATOMS = 625
        N_EDGES = 20000
        ATOM_DIM = 16
        BOND_DIM = 16
        E = bond_features.shape[0]
        d = atom_features.shape[-1]
        bond_mats = (bond_features @ kernel + bias).reshape(E, d, d)
        neigh = atom_features[pair_indices[:, 1]]
        msgs = jnp.einsum('eij,ej->ei', bond_mats, neigh)
        aggregated = jax.ops.segment_sum(msgs, pair_indices[:, 0], num_segments=atom_features.shape[0])
        return aggregated
    edge_index = jnp.stack([src, dst])
    edge_index_t = jnp.stack([src, dst], axis=1)
    x = _layernorm(x + _L0_gnn_ref(x, edge_index, L0_gnn_W_tp, L0_gnn_weight, L0_gnn_bias), axis=-1)
    x = _layernorm(x + _L1_gnn_ref(x, edge_attr_16, edge_index_t, L1_gnn_kernel, L1_gnn_bias), axis=-1)
    return x

_drawn_inputs = setup_inputs


def setup_inputs(seed=0):
    import zlib

    import numpy as np

    out = dict(_drawn_inputs(seed))
    spreads = {'L0_gnn_bias': (0.0, 0.1), 'L1_gnn_bias': (0.0, 0.1)}
    factors = {}
    for name, (base, spread) in spreads.items():
        noise = np.random.default_rng([zlib.crc32(name.encode()), seed]).standard_normal(out[name].shape)
        drawn = base * np.exp(spread * noise) if base else spread * noise
        out[name] = jnp.asarray(drawn.astype(out[name].dtype))
    for name, factor in factors.items():
        out[name] = (out[name] * factor).astype(out[name].dtype)
    return out
```

```python
import concourse.bass as bass
from concourse import mybir
from contextlib import ExitStack


def bass_gnn_resnorm_two_layers(
    nc: bass.Bass,
    x: bass.AP,
    src: bass.AP,
    dst: bass.AP,
    edge_T: bass.AP,
    tp_T: bass.AP,
    weight_T: bass.AP,
    bias0: bass.AP,
    kern: bass.AP,
    bias1: bass.AP,
    out: bass.AP,
):
    F32, F16, I32, I16 = mybir.dt.float32, mybir.dt.float16, mybir.dt.int32, mybir.dt.int16
    U32 = mybir.dt.uint32
    ALU, ACT, AX = mybir.AluOpType, mybir.ActivationFunctionType, mybir.AxisListType
    ABSMAX = bass.bass_isa.ReduceOp.max

    N, C = x.shape
    E = src.shape[0]
    P = 125
    T = 25
    BE = P * T
    NB = E // BE
    U = 3
    NJ = NB // U
    CHUNKS = [4, 4, 4, 4, 3, 3, 3]
    START = [sum(CHUNKS[:k]) for k in range(len(CHUNKS))]
    NK = len(CHUNKS)
    CM = max(CHUNKS)
    WIN = 128
    LO = 8
    HI = 392
    S = 32
    NP = HI * LO // S
    A = S // LO
    ACT_TILES = [[2] * NK, [2] * NK]
    CR = U * NK
    assert NB * BE == E and NB % U == 0 and (U * NK) % 3 == 0 and NP * S == HI * LO >= N

    FB, FW = 120, E * C // 120
    EXP = 0x7F800000
    TOP = (127 + 14 + 127) << 23
    X1S = float(2 ** 12)
    MSGS = float(2.0 ** -37)

    dst16_d = nc.dram_tensor("dst16_scratch", [NB, BE], I16, kind="Internal").ap()
    w0_d = nc.dram_tensor("window_scratch", [2, NB], F32, kind="Internal").ap()
    xtab_d = [nc.dram_tensor(f"node_parts{l}", [NP * S, 2 * C], F16, kind="Internal").ap() for l in range(2)]
    ef_d = nc.dram_tensor("edge_parts", [2 * C, E], F16, kind="Internal").ap()

    ctx = ExitStack()
    with ctx:
        def sb(name, shape, dt):
            return ctx.enter_context(nc.sbuf_tensor(name, shape, dt))

        def sem(name):
            return ctx.enter_context(nc.semaphore(name))

        w0s = sb("w0s", [NB, 2], F32)
        w0b = sb("w0b", [WIN, 2, NB], F32)
        span = sb("span", [WIN, NB], F32)
        spanmax = sb("spanmax", [1, 1], F32)
        npass = sb("npass", [1, 4], I32)
        pcol = sb("pcol", [128, 1], F32)
        ident = sb("ident", [128, 128], F32)
        lo_of_p = sb("lo_of_p", [128, LO], F32)
        iota_hi = sb("iota_hi", [P, HI], F16)
        iota_lo = sb("iota_lo", [P, 2 * LO], I32)
        zeros = sb("zeros", [P, 512], F16)
        wnode = [sb(f"wnode{l}", [WIN, NB], F32) for l in range(2)]
        widxf = [sb(f"widxf{l}", [WIN, NB], F32) for l in range(2)]
        widx = [sb(f"widx{l}", [WIN, NB], I32) for l in range(2)]
        widx_cur = sb("widx_cur", [WIN, U], I32)
        win = sb("win", [WIN, U, 2 * C], F16)
        dstb = sb("dstb", [WIN, U, BE], I16)
        woh = sb("woh", [WIN, U, BE], F16)
        srcr = sb("srcr", [P, U, T], I32)
        lor = sb("lor", [P, U, T], I32)
        hi8 = sb("hi8", [P, U, T], F32)
        nhi8 = sb("nhi8", [P, U, T], F32)
        lomask = sb("lomask", [P, U, T, 2 * LO], F16)
        gparts = sb("gparts", [P, U, T, 2 * C], F16)
        gsum = gparts[:].bitcast(F32)
        hoh = sb("hoh", [P, 3, CM, HI], F16)
        habs = sb("habs", [P, max(map(max, ACT_TILES)), HI], F32)
        vst = sb("vst", [P, 3, CM, 2, LO * C], F16)
        PROD = 3 * CM * C * C
        work = sb("work", [128, PROD + PROD // 2], F32)
        prod = work[0:P, 0:PROD].rearrange("p (s t i j) -> p s t i j", s=3, t=CM, i=C)
        half = work[0:P, PROD:].rearrange("p (s t i j) -> p s t i j", s=3, t=CM, i=C)
        msg = sb("msg", [P, 3, CM, C], F32)
        mpart = sb("mpart", [P, 3, 2, CM, C], F16)
        est = sb("est", [4 * C + 2, U, BE + 1], F16)
        dstw = est[0:NB, :, :].rearrange("p u n -> p (u n)")
        dst32, dst16 = dstw[:, 0:2 * BE].bitcast(I32), dstw[:, 2 * BE:3 * BE].bitcast(I16)
        kst = sb("kst", [4 * C + 2, C * C], F16)
        kf = sb("kf", [4 * C + 2, C * C], F32)
        kh = sb("kh", [4 * C + 2, C * C], F16)
        kl = sb("kl", [4 * C + 2, C * C], F16)
        kw = sb("kw", [4 * C + 2, 4], F32)
        ef = sb("ef", [FB, FW], F32)
        eh = sb("eh", [FB, FW], F16)
        elow = ef[:].bitcast(F16).rearrange("p (n w) -> p n w", w=2)[:, :, 0]
        xn = sb("xn", [NP, S, C], F32)
        y = sb("y", [NP, S, C], F32)
        yd = sb("yd", [NP, S, C], F32)
        yq = sb("yq", [NP, S, C], F32)
        xpart = sb("xpart", [NP, S, 2, C], F16)
        st = sb("st", [NP, 4, S], F32)
        accs = sb("accs", [128, HI], F32)
        wtp = sb("wtp", [C, C, C], F32)
        wtr = (hoh[0:C, :, :, :].rearrange("p a b c -> p (a b c)")[:, 0:2 * C * LO * C].bitcast(F32)
               .rearrange("p (u l v) -> p u l v", u=C, l=LO))
        wtt = sb("wtt", [C, C], F32)
        wrep = sb("wrep", [128, C * C], F32)
        wblk = work[:, LO * C * C:2 * LO * C * C].rearrange("p (l n) -> p l n", l=LO)
        b0 = sb("b0", [NP, C], F32)
        tq = work[0:NP, 0:LO * C * C].rearrange("p (l u o) -> p l u o", l=LO, u=C)
        mx = sb("mx", [128, 3], F32)
        mxa = sb("mxa", [128, 3], F32)
        mxe = sb("mxe", [128, 3], I32)
        scl = sb("scl", [128, 3], I32)
        inv = sb("inv", [128, 3], I32)
        outs = sb("outs", [128, 1], F32)
        scf, invf = scl[:].bitcast(F32), inv[:].bitcast(F32)

        ps = ctx.enter_context(nc.psum_tensor("ps", [128, 8, 512], F32))
        acc = ps[:, 0, 0:HI]
        G_SPLIT = 16

        s_in, s_dst, s_bf = sem("s_in"), sem("s_dst"), sem("s_bf")
        s_w0, s_wb, s_d16 = sem("s_w0"), sem("s_wb"), sem("s_d16")
        s_minmax, s_cast = sem("s_minmax"), sem("s_cast")
        s_pool = sem("s_pool")
        s_gp = sem("s_gp")
        s_mx, s_mxa, s_scale = sem("s_mx"), sem("s_mxa"), sem("s_scale")
        s_ready = sem("s_ready")
        s_eh, s_ef = sem("s_eh"), sem("s_ef")
        s_el = sem("s_el")
        s_xpart, s_xtab = sem("s_xpart"), sem("s_xtab")
        s_dv = sem("s_dv")
        s_wt, s_wrep = sem("s_wt"), sem("s_wrep")
        s_wblk = sem("s_wblk")
        s_acc0, s_accs = sem("s_acc0"), sem("s_accs")
        s_q, s_qd = sem("s_q"), sem("s_qd")
        s_var, s_std = sem("s_var"), sem("s_std")
        s_y, s_out = sem("s_y"), sem("s_out")
        s_sp_waits, s_pool_waits = sem("s_sp_waits"), sem("s_pool_waits")

        class Layer:
            def __init__(self, l):
                def slots(name):
                    return [sem(f"{name}{l}_{i}") for i in range(U)]
                self.l = l
                self.dst_in, self.src_in, self.edge_in = slots("dst_in"), slots("src_in"), slots("edge_in")
                self.win_in = slots("win_in")
                self.zeroed = sem(f"zeroed{l}")
                self.idx_cur = sem(f"idx_cur{l}")
                self.idx_next = sem(f"idx_next{l}")
                self.woh_ready = sem(f"woh_ready{l}")
                self.lo_ready = sem(f"lo_ready{l}")
                self.mask_ready = sem(f"mask_ready{l}")
                self.gathered = sem(f"gathered{l}")
                self.g_copied = sem(f"g_copied{l}")
                self.abs_ready = sem(f"abs_ready{l}")
                self.hoh_act = sem(f"hoh_act{l}")
                self.v_ready = sem(f"v_ready{l}")
                self.scattered = sem(f"scattered{l}")
                self.b_ready = sem(f"b_ready{l}")
                self.prod_ready = sem(f"prod_ready{l}")
                self.half_ready = sem(f"half_ready{l}")
                self.msg_ready = sem(f"msg_ready{l}")
                self.mh_ready = sem(f"mh_ready{l}")
                self.ml_ready = sem(f"ml_ready{l}")
                self.moved = sem(f"moved{l}")
                self.acc_ready = sem(f"acc_ready{l}")

        L = [Layer(0), Layer(1)]

        def block_done(b):
            return b + (1 + U)

        def slot_free(b):
            return b + 1

        def chunk_done(q):
            return q + (1 + CR)

        def ring_free(q):
            return q + (1 + CR - 3)

        def blocks_chunks_free(b):
            return b * NK + NK

        def passes(eng):
            return eng.value_load(npass[0:1, 0:1], min_val=1, max_val=(N + WIN - 1) // WIN)

        def each_block(eng, r, step):
            with eng.Fori(0, NJ - 1) as j:
                for i in range(U):
                    step(j * U + i, r * NB + j * U + i, r * NJ + j, i, False)
            for i in range(U):
                step((NJ - 1) * U + i, r * NB + (NJ - 1) * U + i, r * NJ + (NJ - 1), i, i == U - 1)

        def over_passes(eng, first, step):
            n = passes(eng)
            with eng.Fori(0, n) as r:
                first(r)
                each_block(eng, r, step)

        block = ctx.enter_context(nc.Block())

        @block.sync
        def _(sp):
            sp.dma_start(dst32, dst.rearrange("(b e) -> b e", b=NB)).then_inc(s_dst, 16)
            sp.wait_ge(s_pool, 1)
            sp.dma_start(xn[0:96, :, :], x[0:96 * S, :].rearrange("(p s) c -> p s c", s=S)).then_inc(s_in, 16)
            sp.dma_start(xn[96:97, :, :], x[96 * S:97 * S, :].rearrange("(p s) c -> p s c", s=S)).then_inc(s_in, 16)
            sp.dma_start(xn[97:98, 0:N - 97 * S, :], x[97 * S:N, :].rearrange("(p s) c -> p s c", p=1)).then_inc(s_in, 16)
            for g in range(4):
                sp.dma_start(kf[g * C:(g + 1) * C, :], kern).then_inc(s_in, 16)
            for g in range(2):
                sp.dma_start(kf[4 * C + g:4 * C + g + 1, :], bias1.rearrange("(p n) -> p n", p=1)).then_inc(s_in, 16)
            sp.dma_start(wtp[:], tp_T).then_inc(s_in, 16)
            sp.dma_start(wtt[:], weight_T).then_inc(s_in, 16)
            sp.dma_start(b0[:], bias0.rearrange("(p n) -> p n", p=1).broadcast_to([NP, C])).then_inc(s_in, 16)
            sp.dma_start(ef[:], edge_T.rearrange("c e -> (c e)").rearrange("(p n) -> p n", p=FB)).then_inc(s_bf, 16)
            sp.wait_ge(s_minmax, 1)
            sp.dma_start(w0_d.rearrange("k b -> b k"), w0s[:], allow_slow_non_contiguous=True).then_inc(s_w0, 16)
            sp.wait_ge(s_w0, 16)
            sp.dma_start(w0b[:].rearrange("p k b -> p (k b)"),
                         w0_d.rearrange("k b -> (k b)").rearrange("(o n) -> o n", o=1).broadcast_to([WIN, 2 * NB])
                         ).then_inc(s_wb, 16)
            sp.wait_ge(s_cast, 1)
            sp.dma_start(dst16_d, dst16).then_inc(s_d16, 16)
            sp.wait_ge(s_xpart, 1)
            sp.dma_start(xtab_d[0].rearrange("(p s) c -> p (s c)", s=S),
                         xpart[:].rearrange("p s k c -> p (s k c)")).then_inc(s_xtab, 16)
            sp.wait_ge(s_d16, 16)
            sp.wait_ge(s_ready, 1)

            def loads(z, b, n, u, i):
                sp.wait_ge(z.woh_ready, slot_free(n))
                sp.sem_inc(s_sp_waits, 1)
                sp.dma_start(dstb[:, i, :], dst16_d[bass.ds(b, 1), :].broadcast_to([WIN, BE])
                             ).then_inc(z.dst_in[i], 16)
                sp.wait_ge(z.mask_ready, slot_free(n))
                sp.sem_inc(s_sp_waits, 1)
                sp.dma_start(srcr[:, i, :], src.rearrange("(b p t) -> b p t", b=NB, p=P)[bass.ds(b, 1), :, :]
                             .rearrange("o p t -> (o p) t")).then_inc(z.src_in[i], 16)

            over_passes(sp, lambda r: None, lambda b, n, u, i, last: loads(L[0], b, n, u, i))

            sp.wait_ge(s_ef, 32)
            sp.wait_ge(s_xpart, 2)
            sp.dma_start(xtab_d[1].rearrange("(p s) c -> p (s c)", s=S),
                         xpart[:].rearrange("p s k c -> p (s k c)")).then_inc(s_xtab, 16)

            def loads1(b, n, u, i, last):
                loads(L[1], b, n, u, i)
                sp.wait_ge(L[1].b_ready, blocks_chunks_free(n))
                sp.sem_inc(s_sp_waits, 1)
                for g in range(2):
                    sp.dma_start(est[2 * C * g:2 * C * (g + 1), i, 0:BE], ef_d[:, bass.ds(b * BE, BE)]
                                 ).then_inc(L[1].edge_in[i], 16)

            over_passes(sp, lambda r: None, loads1)
            sp.wait_ge(s_y, 1)
            sp.dma_start(out[0:96 * S, :].rearrange("(p s) c -> p s c", s=S), y[0:96, :, :]).then_inc(s_out, 16)
            sp.dma_start(out[96 * S:97 * S, :].rearrange("(p s) c -> p s c", s=S), y[96:97, :, :]).then_inc(s_out, 16)
            sp.dma_start(out[97 * S:N, :].rearrange("(p s) c -> p s c", p=1), y[97:98, 0:N - 97 * S, :]).then_inc(s_out, 16)
            sp.wait_ge(s_out, 48)
            sp.wait_ge(s_xtab, 32)

        @block.gpsimd
        def _(pool):
            nc.gpsimd.memset(xn[:], 0.0)
            nc.gpsimd.memset(kf[:], 0.0).then_inc(s_pool, 1)
            nc.gpsimd.iota(pcol[:], [[0, 1]], base=0, channel_multiplier=1, allow_small_or_imprecise_dtypes=True)
            nc.gpsimd.iota(iota_hi[:], [[LO, HI]], base=0, channel_multiplier=0, allow_small_or_imprecise_dtypes=True)
            nc.gpsimd.iota(iota_lo[:], [[1, LO], [0, 2]], base=0, channel_multiplier=0)
            nc.gpsimd.memset(ident[:], 0.0)
            nc.gpsimd.memset(lo_of_p[:], 1.0)
            nc.gpsimd.memset(kw[:], 1.0)
            nc.gpsimd.memset(zeros[:], 0.0).then_inc(s_gp, 1)
            pool.wait_ge(s_gp, 1)
            nc.gpsimd.affine_select(out=ident[:], in_=ident[:], compare_op=ALU.not_equal, fill=1.0, base=0,
                                    pattern=[[-1, 128]], channel_multiplier=1)
            nc.gpsimd.affine_select(out=lo_of_p[:], in_=lo_of_p[:], compare_op=ALU.is_ge, fill=0.0, base=0,
                                    pattern=[[-C, LO]], channel_multiplier=1).then_inc(s_gp, 1)
            nc.gpsimd.affine_select(out=kw[:, 0:1], in_=kw[:, 0:1], compare_op=ALU.is_ge, fill=0.0, base=2 * C - 1,
                                    pattern=[[0, 1]], channel_multiplier=-1).then_inc(s_gp, 1)
            pool.wait_ge(s_gp, 3)
            nc.gpsimd.affine_select(out=lo_of_p[:], in_=lo_of_p[:], compare_op=ALU.is_ge, fill=0.0, base=C - 1,
                                    pattern=[[C, LO]], channel_multiplier=-1)
            nc.gpsimd.affine_select(out=kw[:, 0:1], in_=kw[:, 0:1], compare_op=ALU.not_equal, fill=1.0, base=-4 * C,
                                    pattern=[[0, 1]], channel_multiplier=1).then_inc(s_pool, 1)
            pool.wait_ge(s_mx, 1)
            nc.gpsimd.partition_all_reduce(mxa[:], mx[:], 128, ABSMAX).then_inc(s_mxa, 1)

            pool.wait_ge(s_ready, 1)

            def window(z, b, n, u, i):
                pool.wait_ge(z.gathered, slot_free(n))
                pool.sem_inc(s_pool_waits, 1)
                nc.gpsimd.tensor_copy(widx_cur[:, i:i + 1], widx[z.l][:, bass.ds(b, 1)]).then_inc(z.idx_cur, 1)
                pool.wait_ge(z.idx_cur, n + 1)
                pool.sem_inc(s_pool_waits, 1)
                nc.gpsimd.indirect_dma_start(
                    out=win[:, i, :], out_offset=None, in_=xtab_d[z.l],
                    in_offset=bass.IndirectOffsetOnAxis(ap=widx_cur[:, i:i + 1].bitcast(U32), axis=0),
                ).then_inc(z.win_in[i], 16)

            def move(z, r):
                nc.gpsimd.tensor_scalar(widxf[z.l][:], widxf[z.l][:], float(WIN), float(N - 1), ALU.add, ALU.min
                                        ).then_inc(z.idx_next, 1)
                pool.wait_ge(z.idx_next, r * 2 + 1)
                pool.sem_inc(s_pool_waits, 1)
                nc.gpsimd.tensor_copy(widx[z.l][:], widxf[z.l][:]).then_inc(z.idx_next, 1)
                pool.wait_ge(z.idx_next, r * 2 + 2)
                pool.sem_inc(s_pool_waits, 1)

            def halves(q, k, c):
                z = L[1]
                pool.wait_ge(z.prod_ready, chunk_done(q))
                pool.sem_inc(s_pool_waits, 1)
                pool.wait_ge(z.msg_ready, ring_free(q))
                pool.sem_inc(s_pool_waits, 1)
                n = CHUNKS[k]
                nc.gpsimd.tensor_tensor(half[:, c, 0:n, :, :], prod[:, c, 0:n, :, 0:C // 2],
                                        prod[:, c, 0:n, :, C // 2:C], ALU.add).then_inc(z.half_ready, 1)

            def layer(z):
                def step(b, n, u, i, last):
                    if not last:
                        window(z, b + 1, n + 1, u, (i + 1) % U)
                    if z.l:
                        for k in range(NK):
                            halves(n * NK + k, k, (i * NK + k) % 3)

                n = passes(pool)
                with pool.Fori(0, n) as r:
                    window(z, 0, r * NB, r * NJ, 0)
                    each_block(pool, r, step)
                    move(z, r)

            pool.wait_ge(s_xtab, 16)
            layer(L[0])
            pool.wait_ge(s_xtab, 32)
            pool.sem_inc(L[1].half_ready, CR)
            layer(L[1])

        @block.scalar
        def _(act):
            act.wait_ge(s_dst, 16)
            nc.scalar.copy(dst16, dst32).then_inc(s_cast, 1)
            act.wait_ge(s_wrep, 1)
            nc.scalar.copy(wrep[:], ps[:, 2, 0:C * C]).then_inc(s_wrep, 1)
            act.wait_ge(s_scale, 1)
            act.wait_ge(s_bf, 16)
            nc.scalar.activation(eh[:], ef[:], ACT.Copy, scale=scf[0:FB, 1:2]).then_inc(s_eh, 1)
            act.wait_ge(s_eh, 1)
            act.dma_start(ef_d[0:C, :].rearrange("c e -> (c e)").rearrange("(p n) -> p n", p=FB), eh[:]).then_inc(s_ef, 16)
            act.wait_ge(s_ready, 1)

            def copy_gathered(z, n, i):
                act.wait_ge(z.gathered, block_done(n))
                if z.l == 0:
                    act.wait_ge(z.v_ready, blocks_chunks_free(n))
                    nc.scalar.copy(gparts[:, i, 0:G_SPLIT, :],
                                   ps[0:P, 1, 0:G_SPLIT * 2 * C].rearrange("p (t c) -> p t c", t=G_SPLIT))
                    nc.scalar.copy(gparts[:, i, G_SPLIT:T, :],
                                   ps[0:P, 2, 0:(T - G_SPLIT) * 2 * C].rearrange("p (t c) -> p t c", t=T - G_SPLIT)
                                   ).then_inc(z.g_copied, 1)
                else:
                    act.wait_ge(z.prod_ready, blocks_chunks_free(n))
                    nc.scalar.copy(gsum[:, i, :, :], ps[0:P, 1, 0:T * C].rearrange("p (t c) -> p t c", t=T)
                                   ).then_inc(z.g_copied, 1)

            def one_hots(z, n, q, k, i, c):
                m = ACT_TILES[z.l][k]
                if k == 0:
                    act.wait_ge(z.mask_ready, block_done(n))
                act.wait_ge(z.hoh_act, q + CR)
                for a in range(m):
                    t = START[k] + a
                    ins = nc.scalar.activation(habs[:, a, :], iota_hi[:], ACT.Abs, bias=nhi8[:, i, t:t + 1])
                ins.then_inc(z.abs_ready, 1)
                act.wait_ge(z.abs_ready, q + 1)
                act.wait_ge(z.scattered, ring_free(q))
                nc.scalar.activation(hoh[:, c, 0:m, :], habs[:, 0:m, :], ACT.Relu, bias=1.0, scale=-1.0
                                     ).then_inc(z.hoh_act, 1)

            def layer(z):
                act.sem_inc(z.g_copied, U)
                act.sem_inc(z.hoh_act, CR)

                def step(b, n, u, i, last):
                    for k in range(NK):
                        one_hots(z, n, n * NK + k, k, i, (i * NK + k) % 3)
                        if k == 3 and not last:
                            copy_gathered(z, n + 1, (i + 1) % U)

                over_passes(act, lambda r: copy_gathered(z, r * NB, 0), step)

            layer(L[0])
            act.wait_ge(L[0].acc_ready, 1)
            nc.scalar.activation(accs[:], acc, ACT.Copy, scale=invf[:, 0:1]).then_inc(s_accs, 1)
            act.wait_ge(s_el, 1)
            act.wait_ge(s_ef, 16)
            nc.scalar.copy(eh[:], elow).then_inc(s_eh, 1)
            act.wait_ge(s_eh, 2)
            act.dma_start(ef_d[C:2 * C, :].rearrange("c e -> (c e)").rearrange("(p n) -> p n", p=FB), eh[:]).then_inc(s_ef, 16)
            act.wait_ge(s_var, 1)
            nc.scalar.sqrt(st[:, 2, :], st[:, 1, :]).then_inc(s_std, 1)
            layer(L[1])
            act.wait_ge(L[1].acc_ready, 1)
            nc.scalar.activation(accs[:], acc, ACT.Copy, scale=outs[:, 0:1]).then_inc(s_accs, 1)
            act.wait_ge(s_var, 2)
            nc.scalar.sqrt(st[:, 2, :], st[:, 1, :]).then_inc(s_std, 1)

        @block.vector
        def _(dve):
            chain = [0]

            def link(ins):
                chain[0] += 1
                ins.then_inc(s_dv, 1)
                dve.wait_ge(s_dv, chain[0])

            dve.wait_ge(s_dst, 16)
            nc.vector.tensor_reduce(w0s[:, 0:1], dst32, AX.X, ALU.min)
            nc.vector.tensor_reduce(w0s[:, 1:2], dst32, AX.X, ALU.max).then_inc(s_minmax, 1)
            nc.vector.memset(mx[:], 1e-20)
            link(nc.vector.memset(est[4 * C:4 * C + 2, :, :], 1.0))
            dve.wait_ge(s_in, 12 * 16)
            nc.vector.tensor_reduce(mx[0:NP, 0:1], xn[:].rearrange("p s c -> p (s c)"), AX.X, ALU.max,
                                    apply_absolute_value=True)
            nc.vector.tensor_reduce(mx[0:4 * C + 2, 2:3], kf[:], AX.X, ALU.max, apply_absolute_value=True)
            dve.wait_ge(s_bf, 16)
            link(nc.vector.tensor_reduce(mx[0:FB, 1:2], ef[:], AX.X, ALU.max, apply_absolute_value=True))
            link(nc.vector.tensor_scalar(mx[:, 0:1], mx[:, 0:1], 1e-20, None, ALU.max))
            link(nc.vector.tensor_scalar(mx[:, 2:3], mx[:, 2:3], 1e-20, None, ALU.max))
            nc.vector.tensor_scalar(mx[:, 1:2], mx[:, 1:2], 1.0, None, ALU.max).then_inc(s_mx, 1)
            dve.wait_ge(s_mxa, 1)
            link(nc.vector.tensor_single_scalar(mxe[:], mxa[:].bitcast(I32), EXP, ALU.bitwise_and))
            nc.vector.tensor_scalar(inv[:], mxe[:], -float(14 << 23), None, ALU.add)
            link(nc.vector.tensor_scalar(scl[:], mxe[:], -1.0, float(TOP), ALU.mult, ALU.add))
            dve.sem_inc(s_scale, 1)

            def split(values, scale):
                link(nc.vector.tensor_scalar(yd[:], values[:], scale, None, ALU.mult))
                link(nc.vector.tensor_copy(xpart[:, :, 0, :], yd[:]))
                nc.vector.tensor_tensor(xpart[:, :, 1, :], yd[:], xpart[:, :, 0, :], ALU.subtract
                                        ).then_inc(s_xpart, 1)

            split(xn, scf[0:NP, 0:1])
            dve.wait_ge(s_wb, 16)
            dve.wait_ge(s_pool, 2)
            for l in range(2):
                nc.vector.tensor_scalar(wnode[l][:], w0b[:, 0, :], pcol[:, 0:1], None, ALU.add)
                link(nc.vector.tensor_scalar(widxf[l][:], w0b[:, 0, :], pcol[:, 0:1], float(N - 1), ALU.add, ALU.min))
                nc.vector.tensor_copy(widx[l][:], widxf[l][:])
            link(nc.vector.tensor_tensor(span[:], w0b[:, 1, :], w0b[:, 0, :], ALU.subtract))
            link(nc.vector.tensor_reduce(spanmax[:], span[0:1, :], AX.X, ALU.max))
            link(nc.vector.tensor_copy(npass[:, 1:2], spanmax[:]))
            link(nc.vector.tensor_single_scalar(npass[:, 2:3], npass[:, 1:2], 7, ALU.logical_shift_right))
            nc.vector.tensor_scalar(npass[:, 0:1], npass[:, 2:3], 1.0, None, ALU.add).then_inc(s_ready, 1)
            dve.wait_ge(s_ready, 1)
            dve.wait_ge(s_in, 12 * 16)
            nc.vector.tensor_copy(wtr, wtp[:].unsqueeze(2).broadcast_to([C, C, LO, C])).then_inc(s_wt, 1)
            dve.wait_ge(s_wrep, 2)
            for lo in range(LO):
                ins = nc.vector.tensor_scalar(wblk[:, lo, :], wrep[:], lo_of_p[:, lo:lo + 1], None, ALU.mult)
            ins.then_inc(s_wblk, 1)
            link(nc.vector.tensor_scalar(kf[:], kf[:], scf[0:4 * C + 2, 2:3], None, ALU.mult))
            link(nc.vector.tensor_copy(kh[:], kf[:]))
            link(nc.vector.tensor_tensor(kl[:], kf[:], kh[:], ALU.subtract))
            link(nc.vector.tensor_scalar(kw[:, 1:2], kw[:, 0:1], -1.0, 1.0, ALU.mult, ALU.add))
            link(nc.vector.tensor_scalar(kl[:], kl[:], kw[:, 1:2], None, ALU.mult))
            link(nc.vector.scalar_tensor_tensor(kst[:], kh[:], kw[:, 0:1], kl[:], ALU.mult, ALU.add))
            link(nc.vector.tensor_scalar(est[4 * C:4 * C + 2, :, :], est[4 * C:4 * C + 2, :, :],
                                         scf[4 * C:4 * C + 2, 1:2], None, ALU.mult))
            nc.vector.tensor_tensor(outs[:], invf[:, 1:2], invf[:, 2:3], ALU.mult).then_inc(s_dv, 1)
            chain[0] += 1
            dve.wait_ge(s_dv, chain[0])
            link(nc.vector.tensor_scalar(outs[:], outs[:], 1.0 / X1S / MSGS, None, ALU.mult))
            dve.wait_ge(s_eh, 1)
            nc.vector.scalar_tensor_tensor(elow, ef[:], scf[0:FB, 1:2], eh[:], ALU.mult, ALU.subtract).then_inc(s_el, 1)

            def window_one_hot(z, b, n, u, i):
                dve.wait_ge(z.dst_in[i], u * 16 + 16)
                dve.wait_ge(z.gathered, slot_free(n))
                nc.vector.tensor_scalar(woh[:, i, :], dstb[:, i, :], wnode[z.l][:, bass.ds(b, 1)], None, ALU.is_equal
                                        ).then_inc(z.woh_ready, 1)

            def split_src(z, n, u, i):
                dve.wait_ge(z.src_in[i], u * 16 + 16)
                dve.wait_ge(z.hoh_act, blocks_chunks_free(n))
                nc.vector.tensor_single_scalar(lor[:, i, :], srcr[:, i, :], LO - 1, ALU.bitwise_and
                                               ).then_inc(z.lo_ready, 1)
                dve.wait_ge(z.lo_ready, n + 1)
                nc.vector.tensor_tensor(hi8[:, i, :], srcr[:, i, :], lor[:, i, :], ALU.subtract)
                nc.vector.tensor_tensor(nhi8[:, i, :], lor[:, i, :], srcr[:, i, :], ALU.subtract)
                nc.vector.tensor_tensor(lomask[:, i, :, :], lor[:, i, :].unsqueeze(2).broadcast_to([P, T, 2 * LO]),
                                        iota_lo[:].unsqueeze(1).broadcast_to([P, T, 2 * LO]), ALU.is_equal
                                        ).then_inc(z.mask_ready, 1)

            def one_hots(z, q, k, i, c):
                dve.wait_ge(z.scattered, ring_free(q))
                for a in range(ACT_TILES[z.l][k], CHUNKS[k]):
                    t = START[k] + a
                    nc.vector.tensor_scalar(hoh[:, c, a, :], iota_hi[:], hi8[:, i, t:t + 1], None, ALU.is_equal)

            def spread(z, k, i, c, parts):
                t, n = START[k], CHUNKS[k]
                mask = (lomask[:, i, t:t + n, :].rearrange("p t (l w) -> p t l w", w=2).unsqueeze(3)
                        .broadcast_to([P, n, LO, C // 2, 2]))
                for g in range(2):
                    part = parts[g].rearrange("p t (c w) -> p t c w", w=2).unsqueeze(2).broadcast_to([P, n, LO, C // 2, 2])
                    ins = nc.vector.tensor_tensor(
                        vst[:, c, 0:n, g, :].rearrange("p t (l c w) -> p t l c w", l=LO, w=2), part, mask, ALU.mult)
                ins.then_inc(z.v_ready, 1)

            def products(n, q, k, i, c):
                z = L[1]
                if k == 0:
                    dve.wait_ge(z.g_copied, block_done(n))
                dve.wait_ge(z.b_ready, chunk_done(q))
                dve.wait_ge(z.half_ready, ring_free(q))
                t, m = START[k], CHUNKS[k]
                for h in range(0, m, 2):
                    w = min(2, m - h)
                    ins = nc.vector.tensor_tensor(
                        prod[:, c, h:h + w, :, :],
                        ps[0:P, 2 + 2 * c + h // 2, 0:w * C * C].rearrange("p (t i j) -> p t i j", t=w, i=C),
                        gsum[:, i, t + h:t + h + w, :].unsqueeze(2).broadcast_to([P, w, C, C]), ALU.mult)
                ins.then_inc(z.prod_ready, 1)

            def messages(q, k, c):
                z = L[1]
                m = CHUNKS[k]
                dve.wait_ge(z.half_ready, chunk_done(q))
                nc.vector.tensor_reduce(msg[:, c, 0:m, :], half[:, c, 0:m, :, :], AX.X, ALU.add).then_inc(z.msg_ready, 1)
                dve.wait_ge(z.msg_ready, chunk_done(q))
                nc.vector.tensor_scalar(mpart[:, c, 0, 0:m, :], msg[:, c, 0:m, :], MSGS, None, ALU.mult
                                        ).then_inc(z.mh_ready, 1)
                dve.wait_ge(z.mh_ready, q + 1)
                nc.vector.scalar_tensor_tensor(mpart[:, c, 1, 0:m, :], msg[:, c, 0:m, :], MSGS, mpart[:, c, 0, 0:m, :],
                                               ALU.mult, ALU.subtract).then_inc(z.ml_ready, 1)
                dve.wait_ge(z.ml_ready, q + 1)

            def layer(z):
                dve.sem_inc(z.woh_ready, U)
                dve.sem_inc(z.mask_ready, U)
                dve.sem_inc(z.v_ready, CR)
                dve.sem_inc(z.prod_ready, CR)
                dve.sem_inc(z.msg_ready, CR)

                def step(b, n, u, i, last):
                    for k in range(NK):
                        q, c = n * NK + k, (i * NK + k) % 3
                        if k == 0:
                            if not last:
                                u1 = u + 1 if i == U - 1 else u
                                window_one_hot(z, b + 1, n + 1, u1, (i + 1) % U)
                                split_src(z, n + 1, u1, (i + 1) % U)
                            dve.wait_ge(z.mask_ready, block_done(n))
                            if z.l == 0:
                                dve.wait_ge(z.g_copied, block_done(n))
                        if z.l:
                            if k < NK - 1:
                                products(n, q + 1, k + 1, i, (c + 1) % 3)
                            elif not last:
                                products(n + 1, q + 1, 0, (i + 1) % U, (c + 1) % 3)
                        one_hots(z, q, k, i, c)
                        if z.l:
                            messages(q, k, c)
                            spread(z, k, i, c, [mpart[:, c, g, 0:CHUNKS[k], :] for g in range(2)])
                        else:
                            t = START[k]
                            spread(z, k, i, c, [gparts[:, i, t:t + CHUNKS[k], g * C:(g + 1) * C] for g in range(2)])

                def first(r):
                    n = r * NB
                    window_one_hot(z, 0, n, r * NJ, 0)
                    split_src(z, n, r * NJ, 0)
                    if z.l:
                        products(n, n * NK, 0, 0, 0)

                cnt = passes(dve)
                with dve.Fori(0, cnt) as r:
                    first(r)
                    each_block(dve, r, step)
                    nc.vector.tensor_scalar(wnode[z.l][:], wnode[z.l][:], float(WIN), None, ALU.add).then_inc(z.moved, 1)
                    dve.wait_ge(z.moved, r + 1)

            def layer_norm(res, which):
                link(nc.vector.tensor_reduce(st[:, 0, :], y[:], AX.X, ALU.add))
                link(nc.vector.tensor_scalar(st[:, 0, :], st[:, 0, :], 1.0 / C, None, ALU.mult))
                link(nc.vector.tensor_tensor(yd[:], y[:], st[:, 0, :].unsqueeze(2).broadcast_to([NP, S, C]), ALU.subtract))
                link(nc.vector.tensor_tensor(yq[:], yd[:], yd[:], ALU.mult))
                link(nc.vector.tensor_reduce(st[:, 1, :], yq[:], AX.X, ALU.add))
                nc.vector.tensor_scalar(st[:, 1, :], st[:, 1, :], 1.0 / C, 1e-5, ALU.mult, ALU.add).then_inc(s_var, 1)
                dve.wait_ge(s_std, which)
                link(nc.vector.reciprocal(st[:, 3, :], st[:, 2, :]))
                return nc.vector.tensor_tensor(res[:], yd[:], st[:, 3, :].unsqueeze(2).broadcast_to([NP, S, C]), ALU.mult)

            layer(L[0])
            for a in range(A):
                dve.wait_ge(s_q, a + 1)
                for h in range(4):
                    ins = nc.vector.tensor_tensor(
                        tq[:, 2 * h:2 * h + 2, :, :],
                        ps[0:NP, 2 + h, :].rearrange("p (l u o) -> p l u o", l=2, u=C),
                        xn[:, a * LO + 2 * h:a * LO + 2 * h + 2, :].unsqueeze(3).broadcast_to([NP, 2, C, C]), ALU.mult)
                ins.then_inc(s_qd, 1)
                dve.wait_ge(s_qd, a + 1)
                link(nc.vector.tensor_reduce(yq[:, a * LO:(a + 1) * LO, :], tq.rearrange("p l u o -> p l o u"), AX.X, ALU.add))
            link(nc.vector.tensor_tensor(y[:], xn[:], yq[:], ALU.add))
            link(nc.vector.tensor_tensor(y[:], y[:], b0[:].unsqueeze(1).broadcast_to([NP, S, C]), ALU.add))
            link(layer_norm(xn, 1))
            dve.wait_ge(s_xtab, 16)
            split(xn, X1S)
            layer(L[1])
            for a in range(A):
                dve.wait_ge(s_q, A + a + 1)
                link(nc.vector.tensor_tensor(y[:, a * LO:(a + 1) * LO, :], xn[:, a * LO:(a + 1) * LO, :],
                                             ps[0:NP, 2 + a, 0:128].rearrange("p (l c) -> p l c", l=LO), ALU.add))
            layer_norm(y, 2).then_inc(s_y, 1)

        @block.tensor
        def _(pe):
            pe.wait_ge(s_wt, 1)
            for u in range(C):
                ins = nc.tensor.matmul(ps[:, 2, u * C:(u + 1) * C], wtr[:, u, :, :].rearrange("w l v -> w (l v)"),
                                       wtt[:], start=True, stop=True)
            ins.then_inc(s_wrep, 1)
            pe.wait_ge(s_ready, 1)

            def gather(z, n, u, i):
                pe.wait_ge(z.woh_ready, block_done(n))
                pe.wait_ge(z.win_in[i], u * 16 + 16)
                pe.wait_ge(z.g_copied, n + U)
                for t in range(T):
                    edges = woh[:, i, t:BE:T]
                    if z.l == 0:
                        bank, at = (1, t) if t < G_SPLIT else (2, t - G_SPLIT)
                        ins = nc.tensor.matmul(ps[0:P, bank, at * 2 * C:(at + 1) * 2 * C], edges, win[:, i, :],
                                               start=True, stop=True)
                    else:
                        for g in range(2):
                            ins = nc.tensor.matmul(ps[0:P, 1, t * C:(t + 1) * C], edges, win[:, i, g * C:(g + 1) * C],
                                                   start=(g == 0), stop=(g == 1))
                ins.then_inc(z.gathered, 1)

            def edge_matrices(z, n, u, q, k, i, c):
                if k == 0:
                    pe.wait_ge(z.edge_in[i], u * 32 + 32)
                pe.wait_ge(z.prod_ready, ring_free(q))
                for a in range(CHUNKS[k]):
                    t = START[k] + a
                    ins = nc.tensor.matmul(ps[0:P, 2 + 2 * c + a // 2, (a % 2) * C * C:(a % 2 + 1) * C * C],
                                           est[:, i, t * P:(t + 1) * P], kst[:], start=True, stop=True)
                ins.then_inc(z.b_ready, 1)

            def scatter(z, q, k, c):
                pe.wait_ge(z.v_ready, chunk_done(q))
                pe.wait_ge(z.hoh_act, chunk_done(q))
                for a in range(CHUNKS[k]):
                    for g in range(2):
                        ins = nc.tensor.matmul(acc, vst[:, c, a, g, :], hoh[:, c, a, :], start=False, stop=False,
                                               skip_group_check=True)
                ins.then_inc(z.scattered, 1)

            def layer(z):
                pe.sem_inc(z.gathered, U)
                pe.sem_inc(z.scattered, CR)
                pe.sem_inc(z.b_ready, CR)
                nc.tensor.matmul(acc, zeros[:, 0:128], zeros[:, 0:HI], start=True, stop=False, skip_group_check=True)

                def first(r):
                    gather(z, r * NB, r * NJ, 0)
                    if z.l:
                        for k in range(2):
                            edge_matrices(z, r * NB, r * NJ, r * NB * NK + k, k, 0, k)

                def step(b, n, u, i, last):
                    u1 = u + 1 if i == U - 1 else u
                    for k in range(NK):
                        q, c = n * NK + k, (i * NK + k) % 3
                        if k == 1 and not last:
                            gather(z, n + 1, u1, (i + 1) % U)
                        if z.l:
                            if k + 2 < NK:
                                edge_matrices(z, n, u, q + 2, k + 2, i, (c + 2) % 3)
                            elif not last:
                                edge_matrices(z, n + 1, u1, q + 2, k + 2 - NK, (i + 1) % U, (c + 2) % 3)
                        scatter(z, q, k, c)

                over_passes(pe, first, step)
                nc.tensor.matmul(acc, zeros[:, 0:128], zeros[:, 0:HI], start=False, stop=True, skip_group_check=True
                                 ).then_inc(z.acc_ready, 1)

            layer(L[0])
            pe.wait_ge(s_accs, 1)
            pe.wait_ge(s_wblk, 1)
            for a in range(A):
                if a:
                    pe.wait_ge(s_qd, a)
                for h in range(4):
                    ins = nc.tensor.matmul(ps[0:NP, 2 + h, :], accs[:, a:HI:A],
                                           wblk.rearrange("p l n -> p (l n)")[:, h * 512:(h + 1) * 512],
                                           start=True, stop=True)
                ins.then_inc(s_q, 1)
            pe.wait_ge(s_qd, A)
            layer(L[1])
            pe.wait_ge(s_accs, 2)
            for a in range(A):
                nc.tensor.transpose(ps[0:NP, 2 + a, 0:128], accs[:, a:HI:A], ident[:]).then_inc(s_q, 1)


def kernel(x, src, dst, edge_attr_16, L0_gnn_W_tp, L0_gnn_weight, L0_gnn_bias, L1_gnn_kernel, L1_gnn_bias):
    import numpy as _np
    import concourse.bacc as _bacc
    from concourse import mybir as _mybir
    from concourse.bass_utils import run_bass_kernel_spmd as _run

    edge = _np.asarray(edge_attr_16).reshape(33, 125, 25, 16).transpose(3, 0, 2, 1).reshape(16, 103125)
    laid = {
        "x": _np.asarray(x),
        "src": _np.asarray(src),
        "dst": _np.asarray(dst),
        "edge": edge,
        "tp": _np.asarray(L0_gnn_W_tp).transpose(2, 0, 1),
        "weight": _np.asarray(L0_gnn_weight).transpose(1, 0),
        "bias0": _np.asarray(L0_gnn_bias),
        "kern": _np.asarray(L1_gnn_kernel),
        "bias1": _np.asarray(L1_gnn_bias),
    }
    nc = _bacc.Bacc("TRN2", target_bir_lowering=False, num_devices=1)
    arrays, args = {}, []
    for name, a in laid.items():
        a = _np.ascontiguousarray(a)
        arrays[f"in_{name}_dram"] = a
        args.append(nc.dram_tensor(f"in_{name}_dram", a.shape, _mybir.dt.from_np(a.dtype), kind="ExternalInput").ap())
    args.append(nc.dram_tensor("out_0_dram", (3125, 16), _mybir.dt.float32, kind="ExternalOutput").ap())
    bass_gnn_resnorm_two_layers(nc, *args)
    r = _run(nc, [arrays], core_ids=[0])
    return r.results[0]["out_0_dram"]
```

```python
import concourse.bass as bass
from concourse import mybir
from contextlib import ExitStack


def bass_gnn_resnorm_two_layers(
    nc: bass.Bass,
    x: bass.AP,
    src: bass.AP,
    dst: bass.AP,
    edge_T: bass.AP,
    tp_T: bass.AP,
    weight_T: bass.AP,
    bias0: bass.AP,
    kern: bass.AP,
    bias1: bass.AP,
    out: bass.AP,
):
    BF16 = mybir.dt.bfloat16
    F32, F16, I32, I16 = mybir.dt.float32, mybir.dt.float16, mybir.dt.int32, mybir.dt.int16
    U32 = mybir.dt.uint32
    ALU, ACT, AX = mybir.AluOpType, mybir.ActivationFunctionType, mybir.AxisListType
    ABSMAX = bass.bass_isa.ReduceOp.max

    N, C = x.shape
    E = src.shape[0]
    P = 125
    PF = 128
    T = 25
    BE = P * T
    NB = E // BE
    U = 3
    NJ = NB // U
    CHUNKS = [4, 4, 4, 4, 3, 3, 3]
    START = [sum(CHUNKS[:k]) for k in range(len(CHUNKS))]
    NK = len(CHUNKS)
    CM = max(CHUNKS)
    WIN = 128
    LO = 8
    HI = 392
    S = 32
    NP = HI * LO // S
    A = S // LO
    ACT_TILES = [[2, 1, 2, 1, 2, 1, 1], [3, 3, 3, 3, 2, 2, 2]]
    CR = U * NK
    assert NB * BE == E and NB % U == 0 and (U * NK) % 3 == 0 and NP * S == HI * LO >= N

    EW = BE * C // P
    R = 3 * C
    EXP, ONE = 0x7F800000, 1 << 23
    TOP = (127 + 14 + 127) * ONE
    X1S = float(2 ** 12)
    MSGX = 23

    dst16_d = nc.dram_tensor("dst16_scratch", [NB, BE], I16, kind="Internal").ap()
    w0_d = nc.dram_tensor("window_scratch", [2, NB], F32, kind="Internal").ap()
    xtab_d = [nc.dram_tensor(f"node_parts{l}", [NP * S, 2 * C], F16, kind="Internal").ap() for l in range(2)]
    ef_d = nc.dram_tensor("edge_parts", [R, E], BF16, kind="Internal").ap()

    ctx = ExitStack()
    with ctx:
        def sb(name, shape, dt):
            return ctx.enter_context(nc.sbuf_tensor(name, shape, dt))

        def sem(name):
            return ctx.enter_context(nc.semaphore(name))

        w0s = sb("w0s", [NB, 2], F32)
        w0b = sb("w0b", [WIN, 2, NB], F32)
        span = sb("span", [WIN, NB], F32)
        spanmax = sb("spanmax", [1, 1], F32)
        npass = sb("npass", [1, 4], I32)
        pcol = sb("pcol", [128, 1], F32)
        ident = sb("ident", [128, 128], F32)
        lo_of_p = sb("lo_of_p", [128, LO], F32)
        iota_hi = sb("iota_hi", [P, HI], F16)
        iota_lo = sb("iota_lo", [P, 2 * LO], I32)
        zeros = sb("zeros", [P, 512], F16)
        wnode = [sb(f"wnode{l}", [WIN, NB], F32) for l in range(2)]
        widxf = [sb(f"widxf{l}", [WIN, NB], F32) for l in range(2)]
        widx = [sb(f"widx{l}", [WIN, NB], I32) for l in range(2)]
        widx_cur = sb("widx_cur", [WIN, U], I32)
        win = sb("win", [WIN, U, 2 * C], F16)
        dstb = sb("dstb", [WIN, U, BE], I16)
        woh = sb("woh", [WIN, U, BE + PF - P], F16)
        srcr = sb("srcr", [P, U, T], I32)
        lor = sb("lor", [P, U, T], I32)
        hi8 = sb("hi8", [P, U, T], F32)
        nhi8 = sb("nhi8", [P, U, T], F32)
        lomask = sb("lomask", [P, U, T, 2 * LO], F16)
        gparts = sb("gparts", [P, U, T, 2 * C], F16)
        gsum = gparts[:].bitcast(F32)
        hoh = sb("hoh", [P, 3, CM, HI], F16)
        habs = sb("habs", [P, max(map(max, ACT_TILES)), HI], F32)
        vst = sb("vst", [P, 3, CM, 2, LO * C], F16)
        PROD, HALF = 3 * CM * C * C, CM * C * C // 2
        work = sb("work", [128, PROD + HALF + 3 * CM * C * C // 4], F32)
        prod = work[0:P, 0:PROD].rearrange("p (s t i j) -> p s t i j", s=3, t=CM, i=C)
        half = work[0:P, PROD:PROD + HALF].rearrange("p (t i j) -> p t i j", t=CM, i=C)
        quart = work[0:P, PROD + HALF:].rearrange("p (s t i j) -> p s t i j", s=3, t=CM, i=C)
        msg = sb("msg", [P, 3, CM, C], F32)
        mscaled = sb("mscaled", [P, 3, CM, C], F32)
        mpart = sb("mpart", [P, 3, 2, CM, C], F16)
        est = sb("est", [2 * R + 2, U, BE + PF - P], BF16)
        dstw = est[0:NB, :, :].rearrange("p u n -> p (u n)")
        dst32, dst16 = dstw[:, 0:2 * BE].bitcast(I32), dstw[:, 2 * BE:3 * BE].bitcast(I16)
        kst = sb("kst", [2 * R + 2, C * C], F16)
        kf = sb("kf", [2 * R + 2, C * C], F32)
        kh = sb("kh", [2 * R + 2, C * C], F16)
        kl = sb("kl", [2 * R + 2, C * C], F16)
        kw = sb("kw", [2 * R + 2, 2], F32)
        efr = sb("efr", [P, U, EW], F32)
        er1 = sb("er1", [P, EW], F32)
        er2 = sb("er2", [P, EW], F32)
        eparts = sb("eparts", [P, 3, EW], BF16)
        xn = sb("xn", [NP, S, C], F32)
        y = sb("y", [NP, S, C], F32)
        yd = sb("yd", [NP, S, C], F32)
        yq = sb("yq", [NP, S, C], F32)
        xpart = sb("xpart", [NP, S, 2, C], F16)
        st = sb("st", [NP, 4, S], F32)
        accs = sb("accs", [128, HI], F32)
        wtp = sb("wtp", [C, C, C], F32)
        wtr = (hoh[0:C, :, :, :].rearrange("p a b c -> p (a b c)")[:, 0:2 * C * LO * C].bitcast(F32)
               .rearrange("p (u l v) -> p u l v", u=C, l=LO))
        wtt = sb("wtt", [C, C], F32)
        wrep = sb("wrep", [128, C * C], F32)
        wblk = work[:, LO * C * C:2 * LO * C * C].rearrange("p (l n) -> p l n", l=LO)
        b0 = sb("b0", [NP, C], F32)
        tq = work[0:NP, 0:LO * C * C].rearrange("p (l u o) -> p l u o", l=LO, u=C)
        mx = sb("mx", [128, 2], F32)
        mxa = sb("mxa", [128, 2], F32)
        mxe = sb("mxe", [128, 2], I32)
        scl = sb("scl", [128, 2], I32)
        inv = sb("inv", [128, 2], I32)
        em = sb("em", [P, NB], F32)
        emx = sb("emx", [128, 2], F32)
        eme = sb("eme", [128, 1], I32)
        msc = sb("msc", [128, 2], I32)
        outs = sb("outs", [128, 1], F32)
        scf, invf, mscf = scl[:].bitcast(F32), inv[:].bitcast(F32), msc[:].bitcast(F32)

        ps = ctx.enter_context(nc.psum_tensor("ps", [128, 8, 512], F32))
        acc = ps[:, 0, 0:HI]
        G_SPLIT = 16

        s_in, s_dst, s_wts = sem("s_in"), sem("s_dst"), sem("s_wts")
        s_w0, s_wb, s_d16 = sem("s_w0"), sem("s_wb"), sem("s_d16")
        s_minmax, s_cast = sem("s_minmax"), sem("s_cast")
        s_pool = sem("s_pool")
        s_gp = sem("s_gp")
        s_mx, s_mxa, s_scale = sem("s_mx"), sem("s_mxa"), sem("s_scale")
        s_ready = sem("s_ready")
        s_ef, s_em, s_ema = sem("s_ef"), sem("s_em"), sem("s_ema")
        s_xpart, s_xtab = sem("s_xpart"), sem("s_xtab")
        s_dv = sem("s_dv")
        s_wt, s_wrep = sem("s_wt"), sem("s_wrep")
        s_wblk = sem("s_wblk")
        s_acc0, s_accs = sem("s_acc0"), sem("s_accs")
        s_q, s_qd = sem("s_q"), sem("s_qd")
        s_var, s_std = sem("s_var"), sem("s_std")
        s_y, s_out = sem("s_y"), sem("s_out")
        s_sp_waits, s_pool_waits = sem("s_sp_waits"), sem("s_pool_waits")

        class Layer:
            def __init__(self, l):
                def slots(name):
                    return [sem(f"{name}{l}_{i}") for i in range(U)]
                self.l = l
                self.dst_in, self.src_in, self.edge_in = slots("dst_in"), slots("src_in"), slots("edge_in")
                self.win_in = slots("win_in")
                self.ef_in, self.ef_out = slots("ef_in"), slots("ef_out")
                self.zeroed = sem(f"zeroed{l}")
                self.idx_cur = sem(f"idx_cur{l}")
                self.idx_next = sem(f"idx_next{l}")
                self.woh_ready = sem(f"woh_ready{l}")
                self.lo_ready = sem(f"lo_ready{l}")
                self.hi_ready = sem(f"hi_ready{l}")
                self.e_high, self.e_mid = sem(f"e_high{l}"), sem(f"e_mid{l}")
                self.e_rest, self.e_split = sem(f"e_rest{l}"), sem(f"e_split{l}")
                self.e_max = sem(f"e_max{l}")
                self.mask_ready = sem(f"mask_ready{l}")
                self.gathered = sem(f"gathered{l}")
                self.g_copied = sem(f"g_copied{l}")
                self.abs_ready = sem(f"abs_ready{l}")
                self.hoh_act = sem(f"hoh_act{l}")
                self.v_ready = sem(f"v_ready{l}")
                self.scattered = sem(f"scattered{l}")
                self.b_ready = sem(f"b_ready{l}")
                self.prod_ready = sem(f"prod_ready{l}")
                self.half_ready = sem(f"half_ready{l}")
                self.quart_ready = sem(f"quart_ready{l}")
                self.m_scaled = sem(f"m_scaled{l}")
                self.msg_ready = sem(f"msg_ready{l}")
                self.mh_ready = sem(f"mh_ready{l}")
                self.ml_ready = sem(f"ml_ready{l}")
                self.moved = sem(f"moved{l}")
                self.acc_ready = sem(f"acc_ready{l}")

        L = [Layer(0), Layer(1)]

        def block_done(b):
            return b + (1 + U)

        def slot_free(b):
            return b + 1

        def chunk_done(q):
            return q + (1 + CR)

        def ring_free(q):
            return q + (1 + CR - 3)

        def blocks_chunks_free(b):
            return b * NK + NK

        def passes(eng):
            return eng.value_load(npass[0:1, 0:1], min_val=1, max_val=(N + WIN - 1) // WIN)

        def each_block(eng, r, step):
            with eng.Fori(0, NJ - 1) as j:
                for i in range(U):
                    step(j * U + i, r * NB + j * U + i, r * NJ + j, i, False)
            for i in range(U):
                step((NJ - 1) * U + i, r * NB + (NJ - 1) * U + i, r * NJ + (NJ - 1), i, i == U - 1)

        def over_passes(eng, first, step):
            n = passes(eng)
            with eng.Fori(0, n) as r:
                first(r)
                each_block(eng, r, step)

        block = ctx.enter_context(nc.Block())

        @block.sync
        def _(sp):
            sp.dma_start(dst32, dst.rearrange("(b e) -> b e", b=NB)).then_inc(s_dst, 16)
            sp.wait_ge(s_pool, 1)
            sp.dma_start(xn[0:96, :, :], x[0:96 * S, :].rearrange("(p s) c -> p s c", s=S)).then_inc(s_in, 16)
            sp.dma_start(xn[96:97, :, :], x[96 * S:97 * S, :].rearrange("(p s) c -> p s c", s=S)).then_inc(s_in, 16)
            sp.dma_start(xn[97:98, 0:N - 97 * S, :], x[97 * S:N, :].rearrange("(p s) c -> p s c", p=1)).then_inc(s_in, 16)
            for g in range(6):
                sp.dma_start(kf[g * C:(g + 1) * C, :], kern).then_inc(s_in, 16)
            for g in range(2):
                sp.dma_start(kf[2 * R + g:2 * R + g + 1, :], bias1.rearrange("(p n) -> p n", p=1)).then_inc(s_in, 16)
            sp.wait_ge(s_minmax, 1)
            sp.dma_start(w0_d.rearrange("k b -> b k"), w0s[:], allow_slow_non_contiguous=True).then_inc(s_w0, 16)
            sp.wait_ge(s_w0, 16)
            sp.dma_start(w0b[:].rearrange("p k b -> p (k b)"),
                         w0_d.rearrange("k b -> (k b)").rearrange("(o n) -> o n", o=1).broadcast_to([WIN, 2 * NB])
                         ).then_inc(s_wb, 16)
            sp.wait_ge(s_cast, 1)
            sp.dma_start(dst16_d, dst16).then_inc(s_d16, 16)
            sp.dma_start(wtp[:], tp_T).then_inc(s_wts, 16)
            sp.dma_start(wtt[:], weight_T).then_inc(s_wts, 16)
            sp.dma_start(b0[:], bias0.rearrange("(p n) -> p n", p=1).broadcast_to([NP, C])).then_inc(s_wts, 16)
            sp.wait_ge(s_xpart, 1)
            sp.dma_start(xtab_d[0].rearrange("(p s) c -> p (s c)", s=S),
                         xpart[:].rearrange("p s k c -> p (s k c)")).then_inc(s_xtab, 16)
            sp.wait_ge(s_d16, 16)
            sp.wait_ge(s_ready, 1)

            def loads(z, b, n, u, i):
                sp.wait_ge(z.woh_ready, slot_free(n))
                sp.sem_inc(s_sp_waits, 1)
                sp.dma_start(dstb[:, i, :], dst16_d[bass.ds(b, 1), :].broadcast_to([WIN, BE])
                             ).then_inc(z.dst_in[i], 16)
                sp.wait_ge(z.hi_ready, slot_free(n))
                sp.sem_inc(s_sp_waits, 1)
                sp.dma_start(srcr[:, i, :], src.rearrange("(b p t) -> b p t", b=NB, p=P)[bass.ds(b, 1), :, :]
                             .rearrange("o p t -> (o p) t")).then_inc(z.src_in[i], 16)

            def loads0(b, n, u, i, last):
                z = L[0]
                loads(z, b, n, u, i)
                sp.wait_ge(z.e_split, slot_free(n))
                sp.wait_ge(z.e_max, slot_free(n))
                sp.sem_inc(s_sp_waits, 1)
                sp.dma_start(efr[:, i, :], edge_T.rearrange("c e -> (c e)").rearrange("(b p n) -> b p n", b=NB, p=P)
                             [bass.ds(b, 1), :, :].rearrange("o p n -> (o p) n")).then_inc(z.ef_in[i], 16)

            over_passes(sp, lambda r: None, loads0)

            sp.wait_ge(s_ef, 1)
            sp.wait_ge(s_xpart, 2)
            sp.dma_start(xtab_d[1].rearrange("(p s) c -> p (s c)", s=S),
                         xpart[:].rearrange("p s k c -> p (s k c)")).then_inc(s_xtab, 16)

            def loads1(b, n, u, i, last):
                loads(L[1], b, n, u, i)
                sp.wait_ge(L[1].b_ready, blocks_chunks_free(n))
                sp.sem_inc(s_sp_waits, 1)
                for g in range(2):
                    sp.dma_start(est[R * g:R * (g + 1), i, 0:BE], ef_d[:, bass.ds(b * BE, BE)]
                                 ).then_inc(L[1].edge_in[i], 16)

            over_passes(sp, lambda r: None, loads1)
            sp.wait_ge(s_y, 1)
            sp.dma_start(out[0:96 * S, :].rearrange("(p s) c -> p s c", s=S), y[0:96, :, :]).then_inc(s_out, 16)
            sp.dma_start(out[96 * S:97 * S, :].rearrange("(p s) c -> p s c", s=S), y[96:97, :, :]).then_inc(s_out, 16)
            sp.dma_start(out[97 * S:N, :].rearrange("(p s) c -> p s c", p=1), y[97:98, 0:N - 97 * S, :]).then_inc(s_out, 16)
            sp.wait_ge(s_out, 48)
            sp.wait_ge(s_xtab, 32)

        @block.gpsimd
        def _(pool):
            nc.gpsimd.memset(xn[:], 0.0)
            nc.gpsimd.memset(kf[:], 0.0).then_inc(s_pool, 1)
            nc.gpsimd.iota(pcol[:], [[0, 1]], base=0, channel_multiplier=1, allow_small_or_imprecise_dtypes=True)
            nc.gpsimd.iota(iota_hi[:], [[LO, HI]], base=0, channel_multiplier=0, allow_small_or_imprecise_dtypes=True)
            nc.gpsimd.iota(iota_lo[:], [[1, LO], [0, 2]], base=0, channel_multiplier=0)
            nc.gpsimd.memset(ident[:], 0.0)
            nc.gpsimd.memset(lo_of_p[:], 1.0)
            nc.gpsimd.memset(kw[:], 1.0)
            nc.gpsimd.memset(zeros[:], 0.0).then_inc(s_gp, 1)
            pool.wait_ge(s_gp, 1)
            nc.gpsimd.affine_select(out=ident[:], in_=ident[:], compare_op=ALU.not_equal, fill=1.0, base=0,
                                    pattern=[[-1, 128]], channel_multiplier=1)
            nc.gpsimd.affine_select(out=lo_of_p[:], in_=lo_of_p[:], compare_op=ALU.is_ge, fill=0.0, base=0,
                                    pattern=[[-C, LO]], channel_multiplier=1).then_inc(s_gp, 1)
            nc.gpsimd.affine_select(out=kw[:, 0:1], in_=kw[:, 0:1], compare_op=ALU.is_ge, fill=0.0, base=R - 1,
                                    pattern=[[0, 1]], channel_multiplier=-1).then_inc(s_gp, 1)
            pool.wait_ge(s_gp, 3)
            nc.gpsimd.affine_select(out=lo_of_p[:], in_=lo_of_p[:], compare_op=ALU.is_ge, fill=0.0, base=C - 1,
                                    pattern=[[C, LO]], channel_multiplier=-1)
            nc.gpsimd.affine_select(out=kw[:, 0:1], in_=kw[:, 0:1], compare_op=ALU.not_equal, fill=1.0, base=-2 * R,
                                    pattern=[[0, 1]], channel_multiplier=1).then_inc(s_pool, 1)
            pool.wait_ge(s_mx, 1)
            nc.gpsimd.partition_all_reduce(mxa[:], mx[:], 128, ABSMAX).then_inc(s_mxa, 1)

            pool.wait_ge(s_wts, 48)
            nc.gpsimd.tensor_copy(wtr, wtp[:].unsqueeze(2).broadcast_to([C, C, LO, C])).then_inc(s_wt, 1)
            pool.wait_ge(s_ready, 1)

            def window(z, b, n, u, i):
                pool.wait_ge(z.gathered, slot_free(n))
                pool.sem_inc(s_pool_waits, 1)
                nc.gpsimd.tensor_copy(widx_cur[:, i:i + 1], widx[z.l][:, bass.ds(b, 1)]).then_inc(z.idx_cur, 1)
                pool.wait_ge(z.idx_cur, n + 1)
                pool.sem_inc(s_pool_waits, 1)
                nc.gpsimd.indirect_dma_start(
                    out=win[:, i, :], out_offset=None, in_=xtab_d[z.l],
                    in_offset=bass.IndirectOffsetOnAxis(ap=widx_cur[:, i:i + 1].bitcast(U32), axis=0),
                ).then_inc(z.win_in[i], 16)

            def move(z, r):
                nc.gpsimd.tensor_scalar(widxf[z.l][:], widxf[z.l][:], float(WIN), float(N - 1), ALU.add, ALU.min
                                        ).then_inc(z.idx_next, 1)
                pool.wait_ge(z.idx_next, r * 2 + 1)
                pool.sem_inc(s_pool_waits, 1)
                nc.gpsimd.tensor_copy(widx[z.l][:], widxf[z.l][:]).then_inc(z.idx_next, 1)
                pool.wait_ge(z.idx_next, r * 2 + 2)
                pool.sem_inc(s_pool_waits, 1)

            def split_edges(z, b, n, u, i):
                pool.wait_ge(z.ef_in[i], u * 16 + 16)
                pool.sem_inc(s_pool_waits, 1)
                nc.gpsimd.tensor_copy(eparts[:, 0, :], efr[:, i, :]).then_inc(z.e_high, 1)
                pool.wait_ge(z.e_high, n + 1)
                pool.sem_inc(s_pool_waits, 1)
                nc.gpsimd.tensor_tensor(er1[:], efr[:, i, :], eparts[:, 0, :], ALU.subtract).then_inc(z.e_rest, 1)
                pool.wait_ge(z.e_rest, n + 1)
                pool.sem_inc(s_pool_waits, 1)
                nc.gpsimd.tensor_copy(eparts[:, 1, :], er1[:]).then_inc(z.e_mid, 1)
                pool.wait_ge(z.e_mid, n + 1)
                pool.sem_inc(s_pool_waits, 1)
                nc.gpsimd.tensor_tensor(eparts[:, 2, :], er1[:], eparts[:, 1, :], ALU.subtract).then_inc(z.e_split, 1)
                pool.wait_ge(z.e_split, block_done(n))
                pool.sem_inc(s_pool_waits, 1)
                nc.gpsimd.dma_start(
                    ef_d.rearrange("(k c) e -> k (c e)", k=3).rearrange("k (b p n) -> b p k n", b=NB, p=P)
                    [bass.ds(b, 1), :, :, :].rearrange("o p k n -> (o p) k n"), eparts[:]).then_inc(z.ef_out[i], 16)

            def halves(q, k, c):
                z = L[1]
                n = CHUNKS[k]
                pool.wait_ge(z.prod_ready, chunk_done(q))
                pool.wait_ge(z.quart_ready, q + CR)
                pool.sem_inc(s_pool_waits, 1)
                nc.gpsimd.tensor_tensor(half[:, 0:n, :, :], prod[:, c, 0:n, :, 0:C // 2],
                                        prod[:, c, 0:n, :, C // 2:C], ALU.add).then_inc(z.half_ready, 1)
                pool.wait_ge(z.half_ready, chunk_done(q))
                pool.wait_ge(z.msg_ready, ring_free(q))
                pool.sem_inc(s_pool_waits, 1)
                nc.gpsimd.tensor_tensor(quart[:, c, 0:n, :, :], half[:, 0:n, :, 0:C // 4],
                                        half[:, 0:n, :, C // 4:C // 2], ALU.add).then_inc(z.quart_ready, 1)

            def lows(q, k, c):
                z = L[1]
                n = CHUNKS[k]
                pool.wait_ge(z.mh_ready, chunk_done(q))
                pool.wait_ge(z.v_ready, ring_free(q))
                pool.sem_inc(s_pool_waits, 1)
                nc.gpsimd.tensor_tensor(mpart[:, c, 1, 0:n, :], mscaled[:, c, 0:n, :], mpart[:, c, 0, 0:n, :],
                                        ALU.subtract).then_inc(z.ml_ready, 1)

            def layer(z):
                def step(b, n, u, i, last):
                    if not z.l:
                        split_edges(z, b, n, u, i)
                    if not last:
                        u1, i1 = (u + 1 if i == U - 1 else u), (i + 1) % U
                        window(z, b + 1, n + 1, u1, i1)
                    if z.l:
                        for k in range(NK):
                            q, c = n * NK + k, (i * NK + k) % 3
                            if k + 2 < NK or not last:
                                halves(q + 2, (k + 2) % NK, (c + 2) % 3)
                            if k + 1 < NK or not last:
                                lows(q + 1, (k + 1) % NK, (c + 1) % 3)
                    else:
                        pool.wait_ge(z.ef_out[i], u * 16 + 16)
                        pool.sem_inc(s_pool_waits, 1)

                pool.sem_inc(z.e_split, U)
                pool.sem_inc(z.half_ready, CR)
                pool.sem_inc(z.quart_ready, CR)
                pool.sem_inc(z.ml_ready, CR)
                n = passes(pool)
                with pool.Fori(0, n) as r:
                    window(z, 0, r * NB, r * NJ, 0)
                    if z.l:
                        q = r * NB * NK
                        halves(q, 0, 0)
                        halves(q + 1, 1, 1)
                        lows(q, 0, 0)
                    each_block(pool, r, step)
                    move(z, r)

            pool.wait_ge(s_wrep, 2)
            for lo in range(LO):
                ins = nc.gpsimd.tensor_scalar(wblk[:, lo, :], wrep[:], lo_of_p[:, lo:lo + 1], None, ALU.mult)
            ins.then_inc(s_wblk, 1)
            pool.wait_ge(s_xtab, 16)
            layer(L[0])
            pool.sem_inc(s_ef, 1)
            pool.wait_ge(s_em, 1)
            nc.gpsimd.partition_all_reduce(emx[:, 1:2], emx[:, 0:1], 128, ABSMAX).then_inc(s_ema, 1)
            pool.wait_ge(s_xtab, 32)
            layer(L[1])

        @block.scalar
        def _(act):
            act.wait_ge(s_dst, 16)
            nc.scalar.copy(dst16, dst32).then_inc(s_cast, 1)
            act.wait_ge(s_wrep, 1)
            nc.scalar.copy(wrep[:], ps[:, 2, 0:C * C]).then_inc(s_wrep, 1)
            act.wait_ge(s_ready, 1)

            def copy_gathered(z, n, i):
                act.wait_ge(z.gathered, block_done(n))
                if z.l == 0:
                    act.wait_ge(z.v_ready, blocks_chunks_free(n))
                    nc.scalar.copy(gparts[:, i, :, :].rearrange("p t c -> p (t c)"),
                                   ps[0:P, 1:3, :].rearrange("p a n -> p (a n)")[:, 0:T * 2 * C]).then_inc(z.g_copied, 1)
                else:
                    act.wait_ge(z.prod_ready, blocks_chunks_free(n))
                    nc.scalar.copy(gsum[:, i, :, :], ps[0:P, 1, 0:T * C].rearrange("p (t c) -> p t c", t=T)
                                   ).then_inc(z.g_copied, 1)

            def one_hots(z, n, q, k, i, c):
                m = ACT_TILES[z.l][k]
                if k == 0:
                    act.wait_ge(z.hi_ready, block_done(n))
                act.wait_ge(z.hoh_act, q + CR)
                for a in range(m):
                    t = START[k] + a
                    ins = nc.scalar.activation(habs[:, a, :], iota_hi[:], ACT.Abs, bias=nhi8[:, i, t:t + 1])
                ins.then_inc(z.abs_ready, 1)
                act.wait_ge(z.abs_ready, q + 1)
                act.wait_ge(z.scattered, ring_free(q))
                nc.scalar.activation(hoh[:, c, 0:m, :], habs[:, 0:m, :], ACT.Relu, bias=1.0, scale=-1.0
                                     ).then_inc(z.hoh_act, 1)

            def highs(q, k, c):
                z = L[1]
                n = CHUNKS[k]
                act.wait_ge(z.msg_ready, chunk_done(q))
                act.wait_ge(z.ml_ready, ring_free(q))
                nc.scalar.activation(mscaled[:, c, 0:n, :], msg[:, c, 0:n, :], ACT.Copy, scale=mscf[0:P, 0:1])
                act.wait_ge(z.v_ready, ring_free(q))
                nc.scalar.activation(mpart[:, c, 0, 0:n, :], msg[:, c, 0:n, :], ACT.Copy, scale=mscf[0:P, 0:1]
                                     ).then_inc(z.mh_ready, 1)

            def layer(z):
                act.sem_inc(z.g_copied, U)
                act.sem_inc(z.hoh_act, CR)
                act.sem_inc(z.mh_ready, CR)

                def first(r):
                    copy_gathered(z, r * NB, 0)
                    if z.l:
                        highs(r * NB * NK, 0, 0)

                def step(b, n, u, i, last):
                    for k in range(NK):
                        q, c = n * NK + k, (i * NK + k) % 3
                        one_hots(z, n, q, k, i, c)
                        if z.l and (k + 1 < NK or not last):
                            highs(q + 1, (k + 1) % NK, (c + 1) % 3)
                        if k == 3 and not last:
                            copy_gathered(z, n + 1, (i + 1) % U)

                over_passes(act, first, step)

            layer(L[0])
            act.wait_ge(L[0].acc_ready, 1)
            nc.scalar.activation(accs[:], acc, ACT.Copy, scale=invf[:, 0:1]).then_inc(s_accs, 1)
            act.wait_ge(s_var, 1)
            nc.scalar.sqrt(st[:, 2, :], st[:, 1, :]).then_inc(s_std, 1)
            layer(L[1])
            act.wait_ge(L[1].acc_ready, 1)
            nc.scalar.activation(accs[:], acc, ACT.Copy, scale=outs[:, 0:1]).then_inc(s_accs, 1)
            act.wait_ge(s_var, 2)
            nc.scalar.sqrt(st[:, 2, :], st[:, 1, :]).then_inc(s_std, 1)

        @block.vector
        def _(dve):
            chain = [0]

            def link(ins):
                chain[0] += 1
                ins.then_inc(s_dv, 1)
                dve.wait_ge(s_dv, chain[0])

            dve.wait_ge(s_dst, 16)
            nc.vector.tensor_reduce(w0s[:, 0:1], dst32, AX.X, ALU.min)
            nc.vector.tensor_reduce(w0s[:, 1:2], dst32, AX.X, ALU.max).then_inc(s_minmax, 1)
            nc.vector.memset(est[2 * R:2 * R + 2, :, :], 1.0)
            nc.vector.memset(woh[:, :, BE:], 0.0)
            nc.vector.memset(emx[:], 1.0)
            link(nc.vector.memset(mx[:], 1e-20))
            dve.wait_ge(s_in, 11 * 16)
            nc.vector.tensor_reduce(mx[0:NP, 0:1], xn[:].rearrange("p s c -> p (s c)"), AX.X, ALU.max,
                                    apply_absolute_value=True)
            link(nc.vector.tensor_reduce(mx[0:2 * R + 2, 1:2], kf[:], AX.X, ALU.max, apply_absolute_value=True))
            nc.vector.tensor_scalar(mx[:], mx[:], 1e-20, None, ALU.max).then_inc(s_mx, 1)
            dve.wait_ge(s_mxa, 1)
            link(nc.vector.tensor_single_scalar(mxe[:], mxa[:].bitcast(I32), EXP, ALU.bitwise_and))
            nc.vector.tensor_scalar(inv[:], mxe[:], -float(14 * ONE), None, ALU.add)
            link(nc.vector.tensor_scalar(scl[:], mxe[:], -1.0, float(TOP), ALU.mult, ALU.add))

            def split(values, scale):
                link(nc.vector.tensor_scalar(yd[:], values[:], scale, None, ALU.mult))
                link(nc.vector.tensor_copy(xpart[:, :, 0, :], yd[:]))
                nc.vector.tensor_tensor(xpart[:, :, 1, :], yd[:], xpart[:, :, 0, :], ALU.subtract
                                        ).then_inc(s_xpart, 1)

            split(xn, scf[0:NP, 0:1])
            dve.wait_ge(s_wb, 16)
            dve.wait_ge(s_pool, 2)
            for l in range(2):
                nc.vector.tensor_scalar(wnode[l][:], w0b[:, 0, :], pcol[:, 0:1], None, ALU.add)
                link(nc.vector.tensor_scalar(widxf[l][:], w0b[:, 0, :], pcol[:, 0:1], float(N - 1), ALU.add, ALU.min))
                nc.vector.tensor_copy(widx[l][:], widxf[l][:])
            link(nc.vector.tensor_tensor(span[:], w0b[:, 1, :], w0b[:, 0, :], ALU.subtract))
            link(nc.vector.tensor_reduce(spanmax[:], span[0:1, :], AX.X, ALU.max))
            link(nc.vector.tensor_copy(npass[:, 1:2], spanmax[:]))
            link(nc.vector.tensor_single_scalar(npass[:, 2:3], npass[:, 1:2], 7, ALU.logical_shift_right))
            nc.vector.tensor_scalar(npass[:, 0:1], npass[:, 2:3], 1.0, None, ALU.add).then_inc(s_ready, 1)
            dve.wait_ge(s_ready, 1)
            link(nc.vector.tensor_scalar(kf[:], kf[:], scf[0:2 * R + 2, 1:2], None, ALU.mult))
            link(nc.vector.tensor_copy(kh[:], kf[:]))
            link(nc.vector.tensor_tensor(kl[:], kf[:], kh[:], ALU.subtract))
            link(nc.vector.tensor_scalar(kw[:, 1:2], kw[:, 0:1], -1.0, 1.0, ALU.mult, ALU.add))
            link(nc.vector.tensor_scalar(kl[:], kl[:], kw[:, 1:2], None, ALU.mult))
            link(nc.vector.scalar_tensor_tensor(kst[:], kh[:], kw[:, 0:1], kl[:], ALU.mult, ALU.add))

            def window_one_hot(z, b, n, u, i):
                dve.wait_ge(z.dst_in[i], u * 16 + 16)
                dve.wait_ge(z.gathered, slot_free(n))
                nc.vector.tensor_scalar(woh[:, i, 0:BE], dstb[:, i, :], wnode[z.l][:, bass.ds(b, 1)], None, ALU.is_equal
                                        ).then_inc(z.woh_ready, 1)

            def split_src(z, n, u, i):
                dve.wait_ge(z.src_in[i], u * 16 + 16)
                dve.wait_ge(z.hoh_act, blocks_chunks_free(n))
                nc.vector.tensor_single_scalar(lor[:, i, :], srcr[:, i, :], LO - 1, ALU.bitwise_and
                                               ).then_inc(z.lo_ready, 1)
                dve.wait_ge(z.lo_ready, n + 1)
                nc.vector.tensor_tensor(hi8[:, i, :], srcr[:, i, :], lor[:, i, :], ALU.subtract)
                nc.vector.tensor_tensor(nhi8[:, i, :], lor[:, i, :], srcr[:, i, :], ALU.subtract
                                        ).then_inc(z.hi_ready, 1)
                nc.vector.tensor_tensor(lomask[:, i, :, :], lor[:, i, :].unsqueeze(2).broadcast_to([P, T, 2 * LO]),
                                        iota_lo[:].unsqueeze(1).broadcast_to([P, T, 2 * LO]), ALU.is_equal
                                        ).then_inc(z.mask_ready, 1)

            def largest_edge(z, b, n, u, i):
                dve.wait_ge(z.ef_in[i], u * 16 + 16)
                nc.vector.tensor_reduce(em[:, bass.ds(b, 1)], efr[:, i, :], AX.X, ALU.max, apply_absolute_value=True
                                        ).then_inc(z.e_max, 1)

            def one_hots(z, q, k, i, c):
                dve.wait_ge(z.scattered, ring_free(q))
                for a in range(ACT_TILES[z.l][k], CHUNKS[k]):
                    t = START[k] + a
                    nc.vector.tensor_scalar(hoh[:, c, a, :], iota_hi[:], hi8[:, i, t:t + 1], None, ALU.is_equal)

            def spread(z, k, i, c, parts):
                t, n = START[k], CHUNKS[k]
                mask = (lomask[:, i, t:t + n, :].rearrange("p t (l w) -> p t l w", w=2).unsqueeze(3)
                        .broadcast_to([P, n, LO, C // 2, 2]))
                for g in range(2):
                    part = parts[g].rearrange("p t (c w) -> p t c w", w=2).unsqueeze(2).broadcast_to([P, n, LO, C // 2, 2])
                    ins = nc.vector.tensor_tensor(
                        vst[:, c, 0:n, g, :].rearrange("p t (l c w) -> p t l c w", l=LO, w=2), part, mask, ALU.mult)
                ins.then_inc(z.v_ready, 1)

            def products(n, q, k, i, c):
                z = L[1]
                if k == 0:
                    dve.wait_ge(z.g_copied, block_done(n))
                dve.wait_ge(z.b_ready, chunk_done(q))
                dve.wait_ge(z.half_ready, ring_free(q))
                t, m = START[k], CHUNKS[k]
                nc.vector.tensor_tensor(
                    prod[:, c, 0:m, :, :],
                    ps[0:P, 2 + 2 * c:4 + 2 * c, :].rearrange("p a n -> p (a n)")[:, 0:m * C * C]
                    .rearrange("p (t i j) -> p t i j", t=m, i=C),
                    gsum[:, i, t:t + m, :].unsqueeze(2).broadcast_to([P, m, C, C]), ALU.mult).then_inc(z.prod_ready, 1)

            def messages(q, k, c):
                z = L[1]
                m = CHUNKS[k]
                dve.wait_ge(z.quart_ready, chunk_done(q))
                dve.wait_ge(z.mh_ready, ring_free(q))
                nc.vector.tensor_reduce(msg[:, c, 0:m, :], quart[:, c, 0:m, :, :], AX.X, ALU.add
                                        ).then_inc(z.msg_ready, 1)

            def layer(z):
                dve.sem_inc(z.woh_ready, U)
                dve.sem_inc(z.hi_ready, U)
                dve.sem_inc(z.mask_ready, U)
                dve.sem_inc(z.e_max, U)
                dve.sem_inc(z.v_ready, CR)
                dve.sem_inc(z.prod_ready, CR)
                dve.sem_inc(z.msg_ready, CR)

                def step(b, n, u, i, last):
                    u1, i1 = (u + 1 if i == U - 1 else u), (i + 1) % U
                    for k in range(NK):
                        q, c = n * NK + k, (i * NK + k) % 3
                        if k == 0:
                            if not last:
                                window_one_hot(z, b + 1, n + 1, u1, i1)
                                split_src(z, n + 1, u1, i1)
                            dve.wait_ge(z.mask_ready, block_done(n))
                            if z.l == 0:
                                dve.wait_ge(z.g_copied, block_done(n))
                        if z.l:
                            if k + 2 < NK:
                                products(n, q + 2, k + 2, i, (c + 2) % 3)
                            elif not last:
                                products(n + 1, q + 2, k + 2 - NK, i1, (c + 2) % 3)
                            one_hots(z, q, k, i, c)
                            if k + 1 < NK or not last:
                                messages(q + 1, (k + 1) % NK, (c + 1) % 3)
                            dve.wait_ge(z.ml_ready, chunk_done(q))
                            spread(z, k, i, c, [mpart[:, c, g, 0:CHUNKS[k], :] for g in range(2)])
                        else:
                            one_hots(z, q, k, i, c)
                            t = START[k]
                            spread(z, k, i, c, [gparts[:, i, t:t + CHUNKS[k], g * C:(g + 1) * C] for g in range(2)])
                    if not z.l:
                        largest_edge(z, b, n, u, i)

                def first(r):
                    n = r * NB
                    window_one_hot(z, 0, n, r * NJ, 0)
                    split_src(z, n, r * NJ, 0)
                    if z.l:
                        products(n, n * NK, 0, 0, 0)
                        products(n, n * NK + 1, 1, 0, 1)
                        messages(n * NK, 0, 0)

                cnt = passes(dve)
                with dve.Fori(0, cnt) as r:
                    first(r)
                    each_block(dve, r, step)
                    nc.vector.tensor_scalar(wnode[z.l][:], wnode[z.l][:], float(WIN), None, ALU.add).then_inc(z.moved, 1)
                    dve.wait_ge(z.moved, r + 1)

            def layer_norm(res, which):
                link(nc.vector.tensor_reduce(st[:, 0, :], y[:], AX.X, ALU.add))
                link(nc.vector.tensor_scalar(st[:, 0, :], st[:, 0, :], 1.0 / C, None, ALU.mult))
                link(nc.vector.tensor_tensor(yd[:], y[:], st[:, 0, :].unsqueeze(2).broadcast_to([NP, S, C]), ALU.subtract))
                link(nc.vector.tensor_tensor(yq[:], yd[:], yd[:], ALU.mult))
                link(nc.vector.tensor_reduce(st[:, 1, :], yq[:], AX.X, ALU.add))
                nc.vector.tensor_scalar(st[:, 1, :], st[:, 1, :], 1.0 / C, 1e-5, ALU.mult, ALU.add).then_inc(s_var, 1)
                dve.wait_ge(s_std, which)
                link(nc.vector.reciprocal(st[:, 3, :], st[:, 2, :]))
                return nc.vector.tensor_tensor(res[:], yd[:], st[:, 3, :].unsqueeze(2).broadcast_to([NP, S, C]), ALU.mult)

            layer(L[0])
            dve.wait_ge(L[0].e_max, U + 1)
            link(nc.vector.tensor_reduce(emx[0:P, 0:1], em[:], AX.X, ALU.max))
            nc.vector.tensor_scalar(emx[:, 0:1], emx[:, 0:1], 1.0, None, ALU.max).then_inc(s_em, 1)
            for a in range(A):
                dve.wait_ge(s_q, a + 1)
                for h in range(4):
                    ins = nc.vector.tensor_tensor(
                        tq[:, 2 * h:2 * h + 2, :, :],
                        ps[0:NP, 2 + h, :].rearrange("p (l u o) -> p l u o", l=2, u=C),
                        xn[:, a * LO + 2 * h:a * LO + 2 * h + 2, :].unsqueeze(3).broadcast_to([NP, 2, C, C]), ALU.mult)
                ins.then_inc(s_qd, 1)
                dve.wait_ge(s_qd, a + 1)
                link(nc.vector.tensor_reduce(yq[:, a * LO:(a + 1) * LO, :], tq.rearrange("p l u o -> p l o u"), AX.X, ALU.add))
            link(nc.vector.tensor_tensor(y[:], xn[:], yq[:], ALU.add))
            link(nc.vector.tensor_tensor(y[:], y[:], b0[:].unsqueeze(1).broadcast_to([NP, S, C]), ALU.add))
            link(layer_norm(xn, 1))
            dve.wait_ge(s_xtab, 16)
            split(xn, X1S)
            dve.wait_ge(s_ema, 1)
            link(nc.vector.tensor_single_scalar(eme[:], emx[:, 1:2].bitcast(I32), EXP, ALU.bitwise_and))
            nc.vector.tensor_scalar(msc[:, 1:2], eme[:], float(MSGX * ONE), None, ALU.add)
            link(nc.vector.tensor_scalar(msc[:, 0:1], eme[:], -1.0, float((254 - MSGX) * ONE), ALU.mult, ALU.add))
            link(nc.vector.tensor_tensor(outs[:], invf[:, 1:2], mscf[:, 1:2], ALU.mult))
            link(nc.vector.tensor_scalar(outs[:], outs[:], 1.0 / X1S, None, ALU.mult))
            link(nc.vector.memset(est[0:2 * R, :, BE:], 0.0))
            layer(L[1])
            for a in range(A):
                dve.wait_ge(s_q, A + a + 1)
                link(nc.vector.tensor_tensor(y[:, a * LO:(a + 1) * LO, :], xn[:, a * LO:(a + 1) * LO, :],
                                             ps[0:NP, 2 + a, 0:128].rearrange("p (l c) -> p l c", l=LO), ALU.add))
            layer_norm(y, 2).then_inc(s_y, 1)

        @block.tensor
        def _(pe):
            pe.wait_ge(s_wt, 1)
            for u in range(C):
                ins = nc.tensor.matmul(ps[:, 2, u * C:(u + 1) * C], wtr[:, u, :, :].rearrange("w l v -> w (l v)"),
                                       wtt[:], start=True, stop=True)
            ins.then_inc(s_wrep, 1)
            pe.wait_ge(s_ready, 1)

            def gather(z, n, u, i):
                pe.wait_ge(z.woh_ready, block_done(n))
                pe.wait_ge(z.win_in[i], u * 16 + 16)
                pe.wait_ge(z.g_copied, n + U)
                for t in range(T):
                    edges = woh[:, i, t * P:t * P + PF]
                    if z.l == 0:
                        bank, at = (1, t) if t < G_SPLIT else (2, t - G_SPLIT)
                        ins = nc.tensor.matmul(ps[:, bank, at * 2 * C:(at + 1) * 2 * C], edges, win[:, i, :],
                                               start=True, stop=True)
                    else:
                        for g in range(2):
                            ins = nc.tensor.matmul(ps[:, 1, t * C:(t + 1) * C], edges, win[:, i, g * C:(g + 1) * C],
                                                   start=(g == 0), stop=(g == 1))
                ins.then_inc(z.gathered, 1)

            def edge_matrices(z, n, u, q, k, i, c):
                if k == 0:
                    pe.wait_ge(z.edge_in[i], u * 32 + 32)
                pe.wait_ge(z.prod_ready, ring_free(q))
                for a in range(CHUNKS[k]):
                    t = START[k] + a
                    ins = nc.tensor.matmul(ps[:, 2 + 2 * c + a // 2, (a % 2) * C * C:(a % 2 + 1) * C * C],
                                           est[:, i, t * P:t * P + PF], kst[:], start=True, stop=True)
                ins.then_inc(z.b_ready, 1)

            def scatter(z, q, k, c):
                pe.wait_ge(z.v_ready, chunk_done(q))
                pe.wait_ge(z.hoh_act, chunk_done(q))
                for a in range(CHUNKS[k]):
                    for g in range(2):
                        ins = nc.tensor.matmul(acc, vst[:, c, a, g, :], hoh[:, c, a, :], start=False, stop=False,
                                               skip_group_check=True)
                ins.then_inc(z.scattered, 1)

            def layer(z):
                pe.sem_inc(z.gathered, U)
                pe.sem_inc(z.scattered, CR)
                pe.sem_inc(z.b_ready, CR)
                nc.tensor.matmul(acc, zeros[:, 0:128], zeros[:, 0:HI], start=True, stop=False, skip_group_check=True)

                def first(r):
                    gather(z, r * NB, r * NJ, 0)
                    if z.l:
                        for k in range(3):
                            edge_matrices(z, r * NB, r * NJ, r * NB * NK + k, k, 0, k)

                def step(b, n, u, i, last):
                    u1 = u + 1 if i == U - 1 else u
                    for k in range(NK):
                        q, c = n * NK + k, (i * NK + k) % 3
                        if k == 1 and not last:
                            gather(z, n + 1, u1, (i + 1) % U)
                        if z.l:
                            if k + 3 < NK:
                                edge_matrices(z, n, u, q + 3, k + 3, i, c)
                            elif not last:
                                edge_matrices(z, n + 1, u1, q + 3, k + 3 - NK, (i + 1) % U, c)
                        scatter(z, q, k, c)

                over_passes(pe, first, step)
                nc.tensor.matmul(acc, zeros[:, 0:128], zeros[:, 0:HI], start=False, stop=True, skip_group_check=True
                                 ).then_inc(z.acc_ready, 1)

            layer(L[0])
            pe.wait_ge(s_accs, 1)
            pe.wait_ge(s_wblk, 1)
            for a in range(A):
                if a:
                    pe.wait_ge(s_qd, a)
                for h in range(4):
                    ins = nc.tensor.matmul(ps[0:NP, 2 + h, :], accs[:, a:HI:A],
                                           wblk.rearrange("p l n -> p (l n)")[:, h * 512:(h + 1) * 512],
                                           start=True, stop=True)
                ins.then_inc(s_q, 1)
            pe.wait_ge(s_qd, A)
            layer(L[1])
            pe.wait_ge(s_accs, 2)
            for a in range(A):
                nc.tensor.transpose(ps[0:NP, 2 + a, 0:128], accs[:, a:HI:A], ident[:]).then_inc(s_q, 1)


def kernel(x, src, dst, edge_attr_16, L0_gnn_W_tp, L0_gnn_weight, L0_gnn_bias, L1_gnn_kernel, L1_gnn_bias):
    import numpy as _np
    import concourse.bacc as _bacc
    from concourse import mybir as _mybir
    from concourse.bass_utils import run_bass_kernel_spmd as _run

    src_rows = _np.asarray(src).reshape(33, 25, 125).transpose(0, 2, 1).reshape(103125)
    laid = {
        "x": _np.asarray(x),
        "src": src_rows,
        "dst": _np.asarray(dst),
        "edge": _np.asarray(edge_attr_16).transpose(1, 0),
        "tp": _np.asarray(L0_gnn_W_tp).transpose(2, 0, 1),
        "weight": _np.asarray(L0_gnn_weight).transpose(1, 0),
        "bias0": _np.asarray(L0_gnn_bias),
        "kern": _np.asarray(L1_gnn_kernel),
        "bias1": _np.asarray(L1_gnn_bias),
    }
    nc = _bacc.Bacc("TRN2", target_bir_lowering=False, num_devices=1)
    arrays, args = {}, []
    for name, a in laid.items():
        a = _np.ascontiguousarray(a)
        arrays[f"in_{name}_dram"] = a
        args.append(nc.dram_tensor(f"in_{name}_dram", a.shape, _mybir.dt.from_np(a.dtype), kind="ExternalInput").ap())
    args.append(nc.dram_tensor("out_0_dram", (3125, 16), _mybir.dt.float32, kind="ExternalOutput").ap())
    bass_gnn_resnorm_two_layers(nc, *args)
    r = _run(nc, [arrays], core_ids=[0])
    return r.results[0]["out_0_dram"]
```

```python
import concourse.bass as bass
from concourse import mybir
from contextlib import ExitStack


def bass_gnn_resnorm_two_layers(
    nc: bass.Bass,
    x: bass.AP,
    src: bass.AP,
    dst: bass.AP,
    edge_T: bass.AP,
    tp_T: bass.AP,
    weight_T: bass.AP,
    bias0: bass.AP,
    kern: bass.AP,
    bias1: bass.AP,
    out: bass.AP,
):
    BF16 = mybir.dt.bfloat16
    F32, F16, I32, I16 = mybir.dt.float32, mybir.dt.float16, mybir.dt.int32, mybir.dt.int16
    ALU, ACT, AX = mybir.AluOpType, mybir.ActivationFunctionType, mybir.AxisListType
    ABSMAX = bass.bass_isa.ReduceOp.max

    N, C = x.shape
    E = src.shape[0]
    P = 125
    PF = 128
    T = 25
    BE = P * T
    NB = E // BE
    U = 3
    NJ = NB // U
    CHUNKS = [4, 4, 4, 4, 3, 3, 3]
    START = [sum(CHUNKS[:k]) for k in range(len(CHUNKS))]
    NK = len(CHUNKS)
    CM = max(CHUNKS)
    WIN = 128
    LO = 8
    HI = 392
    S = 32
    NP = HI * LO // S
    A = S // LO
    ACT_TILES = [[1, 2, 1, 2, 1, 1, 1], [2, 2, 2, 3, 2, 2, 2]]
    GATHER = [{1: range(T)}, {0: range(0, 17), 1: range(17, T)}]
    KEPT = [0, 1]
    POOL_SUMS = [6]
    DVE_SUMS = [k for k in range(NK) if k not in POOL_SUMS]
    POOL_ONE_HOTS = [5, 6]
    CR = U * NK
    assert NB * BE == E and NB % U == 0 and (U * NK) % 3 == 0 and NP * S == HI * LO >= N

    EW = BE * C // P
    R = 3 * C
    EXP, ONE = 0x7F800000, 1 << 23
    TOP = (127 + 14 + 127) * ONE
    X1S = float(2 ** 12)
    MSGX = 23

    dst16_d = nc.dram_tensor("dst16_scratch", [NB, BE], I16, kind="Internal").ap()
    w0_d = nc.dram_tensor("window_scratch", [2, NB], F32, kind="Internal").ap()
    xtab_d = [nc.dram_tensor(f"node_parts{l}", [NP * S + WIN, 2 * C], F16, kind="Internal").ap() for l in range(2)]
    nodes_d = nc.dram_tensor("nodes_kept", [NB, P, T * 2 * LO * 2 + 2 * T], F16, kind="Internal").ap()
    hoh_d = nc.dram_tensor("one_hots_kept", [NB, NK, P, HI], F16, kind="Internal").ap()
    ef_d = nc.dram_tensor("edge_parts", [R, E], BF16, kind="Internal").ap()

    ctx = ExitStack()
    with ctx:
        def sb(name, shape, dt):
            return ctx.enter_context(nc.sbuf_tensor(name, shape, dt))

        def sem(name):
            return ctx.enter_context(nc.semaphore(name))

        w0s = sb("w0s", [NB, 2], F32)
        w0b = sb("w0b", [WIN, 2, NB], F32)
        span = sb("span", [WIN, NB], F32)
        spanmax = sb("spanmax", [1, 1], F32)
        npass = sb("npass", [1, 4], I32)
        pcol = sb("pcol", [128, 1], F32)
        ident = sb("ident", [128, 128], F32)
        lo_of_p = sb("lo_of_p", [128, LO], F32)
        iota_hi = sb("iota_hi", [P, HI], F16)
        iota_lo = sb("iota_lo", [P, 2 * LO, 2], I16)
        zeros = sb("zeros", [P, 512], F16)
        wnode = [sb(f"wnode{l}", [WIN, NB], F32) for l in range(2)]
        wrowf = [sb(f"wrowf{l}", [1, NB], F32) for l in range(2)]
        wrow = [sb(f"wrow{l}", [1, NB], I32) for l in range(2)]
        win = sb("win", [WIN, U, 2 * C], F16)
        dstb = sb("dstb", [WIN, U, BE], I16)
        woh = sb("woh", [WIN, U, BE + PF - P], F16)
        NM = T * 2 * LO * 2
        nodes = sb("nodes", [P, U, NM + 2 * T], F16)
        lomask = nodes[:, :, 0:NM].rearrange("p u (t l w) -> p u t l w", t=T, w=2)
        hi8 = nodes[:, :, NM:].bitcast(F32)
        srcr = sb("srcr", [P, U, T], I32)
        lor = sb("lor", [P, U, T, 2], I16)
        gparts = sb("gparts", [P, U, T, 2 * C], F16)
        gsum = gparts[:].bitcast(F32)
        hoh = sb("hoh", [P, NK, CM, HI], F16)
        habs = sb("habs", [P, 3, max(map(max, ACT_TILES)), HI], F32)
        vst = sb("vst", [P, NK, CM, 2, LO * C], F16)
        PROD, HALF = NK * CM * C * C, 3 * CM * C * C // 2
        work = sb("work", [128, PROD + HALF + NK * CM * C * C // 4], F32)
        prod = work[0:P, 0:PROD].rearrange("p (s t i j) -> p s t i j", s=NK, t=CM, i=C)
        half = work[0:P, PROD:PROD + HALF].rearrange("p (s t i j) -> p s t i j", s=3, t=CM, i=C)
        quart = work[0:P, PROD + HALF:].rearrange("p (s t i j) -> p s t i j", s=NK, t=CM, i=C)
        eighth = sb("eighth", [P, CM, C, 2], F32)
        msg = sb("msg", [P, NK, CM, C], F32)
        mpart = sb("mpart", [P, NK, CM, 2, C], F16)
        est = sb("est", [2 * R + 2, U, BE + PF - P], BF16)
        dstw = est[0:NB, :, :].rearrange("p u n -> p (u n)")
        dst32, dst16 = dstw[:, 0:2 * BE].bitcast(I32), dstw[:, 2 * BE:3 * BE].bitcast(I16)
        kst = sb("kst", [2 * R + 2, C * C], F16)
        kf = sb("kf", [2 * R + 2, C * C], F32)
        kh = sb("kh", [2 * R + 2, C * C], F16)
        kl = sb("kl", [2 * R + 2, C * C], F16)
        kw = sb("kw", [2 * R + 2, 2], F32)
        efr = sb("efr", [P, U, EW], F32)
        er1 = sb("er1", [P, EW], F32)
        eparts = sb("eparts", [P, 3, EW], BF16)
        xn = sb("xn", [NP, S, C], F32)
        y = sb("y", [NP, S, C], F32)
        yd = sb("yd", [NP, S, C], F32)
        yq = sb("yq", [NP, S, C], F32)
        xpart = sb("xpart", [NP, S, 2, C], F16)
        st = sb("st", [NP, 4, S], F32)
        accs = sb("accs", [128, HI], F32)
        wtp = sb("wtp", [C, C, C], F32)
        wtr = (hoh[0:C, :, :, :].rearrange("p a b c -> p (a b c)")[:, 0:2 * C * LO * C].bitcast(F32)
               .rearrange("p (u l v) -> p u l v", u=C, l=LO))
        wtt = sb("wtt", [C, C], F32)
        wrep = sb("wrep", [128, C * C], F32)
        wblk = work[:, LO * C * C:2 * LO * C * C].rearrange("p (l n) -> p l n", l=LO)
        b0 = sb("b0", [NP, C], F32)
        tq = work[0:NP, 0:LO * C * C].rearrange("p (l u o) -> p l u o", l=LO, u=C)
        mx = sb("mx", [128, 2], F32)
        mxa = sb("mxa", [128, 2], F32)
        mxe = sb("mxe", [128, 2], I32)
        scl = sb("scl", [128, 2], I32)
        inv = sb("inv", [128, 2], I32)
        em = sb("em", [P, NB], F32)
        emx = sb("emx", [128, 2], F32)
        eme = sb("eme", [128, 1], I32)
        msc = sb("msc", [128, 2], I32)
        outs = sb("outs", [128, 1], F32)
        scf, invf, mscf = scl[:].bitcast(F32), inv[:].bitcast(F32), msc[:].bitcast(F32)

        ps = ctx.enter_context(nc.psum_tensor("ps", [128, 8, 512], F32))
        acc = ps[:, 0, 0:HI]
        G_SPLIT = 16
        NODE_BANK = [4, 0]

        s_in, s_dst, s_wts = sem("s_in"), sem("s_dst"), sem("s_wts")
        s_minmax, s_w0, s_wb = sem("s_minmax"), sem("s_w0"), sem("s_wb")
        s_cast, s_d16 = sem("s_cast"), sem("s_d16")
        s_pool = sem("s_pool")
        s_gp = sem("s_gp")
        s_dv = sem("s_dv")
        s_mx, s_mxa = sem("s_mx"), sem("s_mxa")
        s_ready = sem("s_ready")
        s_ef = sem("s_ef")
        s_em, s_ema = sem("s_em"), sem("s_ema")
        s_msc = sem("s_msc")
        s_xpart, s_xtab = sem("s_xpart"), sem("s_xtab")
        s_wt, s_wrep = sem("s_wt"), sem("s_wrep")
        s_wblk = sem("s_wblk")
        s_accs = sem("s_accs")
        s_q, s_qd = sem("s_q"), sem("s_qd")
        s_var, s_std = sem("s_var"), sem("s_std")
        s_y, s_out = sem("s_y"), sem("s_out")
        s_sp_waits, s_pool_waits = sem("s_sp_waits"), sem("s_pool_waits")

        class Layer:
            def __init__(self, l):
                def slots(name):
                    return [sem(f"{name}{l}_{i}") for i in range(U)]
                self.l = l
                self.dst_in, self.src_in, self.edge_in = slots("dst_in"), slots("src_in"), slots("edge_in")
                self.win_in = slots("win_in")
                self.nodes_out, self.nodes_in = slots("nodes_out"), slots("nodes_in")
                self.kept_out = [sem(f"kept_out{l}_{k}") for k in range(NK)] if not l else None
                self.kept_in = [sem(f"kept_in{l}_{k}") for k in range(NK)] if l else None
                self.ef_in, self.ef_out = slots("ef_in"), slots("ef_out")
                self.rows_ready = sem(f"rows_ready{l}")
                self.lo_ready = sem(f"lo_ready{l}")
                self.e_high, self.e_rest, self.e_mid = sem(f"e_high{l}"), sem(f"e_rest{l}"), sem(f"e_mid{l}")
                self.e_split = sem(f"e_split{l}")
                self.woh_ready = sem(f"woh_ready{l}")
                self.hi_ready = sem(f"hi_ready{l}")
                self.e_max = sem(f"e_max{l}")
                self.mask_ready = sem(f"mask_ready{l}")
                self.gathered = sem(f"gathered{l}")
                self.g_copied = sem(f"g_copied{l}")
                self.hoh_pool = sem(f"hoh_pool{l}")
                self.abs_ready = sem(f"abs_ready{l}")
                self.hoh_act = sem(f"hoh_act{l}")
                self.v_ready = sem(f"v_ready{l}")
                self.scattered = sem(f"scattered{l}")
                self.b_ready = sem(f"b_ready{l}")
                self.prod_ready = sem(f"prod_ready{l}")
                self.half_ready = sem(f"half_ready{l}")
                self.quart_ready = sem(f"quart_ready{l}")
                self.mh_ready = sem(f"mh_ready{l}")
                self.ml_ready = sem(f"ml_ready{l}")
                self.eighth_ready = sem(f"eighth_ready{l}")
                self.msg_pool = sem(f"msg_pool{l}")
                self.msg_dve = sem(f"msg_dve{l}")
                self.moved = sem(f"moved{l}")
                self.acc_ready = sem(f"acc_ready{l}")

        L = [Layer(0), Layer(1)]

        def block_done(b):
            return b + (1 + U)

        def slot_free(b):
            return b + 1

        def chunk_done(q):
            return q + (1 + CR)

        def ring_free(q):
            return q + (1 + CR - NK)

        def banks_free(q):
            return q + (1 + CR - 3)

        def blocks_chunks_free(b):
            return b * NK + NK

        def among_done(n, k, some):
            return n * len(some) + (some.index(k) + 1 + len(some))

        def among_free(n, k, some):
            return n * len(some) + (some.index(k) + 1)

        def one_hot_done(n, k):
            return n * len(POOL_ONE_HOTS) + (POOL_ONE_HOTS.index(k) + 1 + U * len(POOL_ONE_HOTS))

        def passes(eng):
            return eng.value_load(npass[0:1, 0:1], min_val=1, max_val=(N + WIN - 1) // WIN)

        def each_block(eng, r, step):
            with eng.Fori(0, NJ - 1) as j:
                for i in range(U):
                    step(j * U + i, r * NB + j * U + i, r * NJ + j, i, U)
            for i in range(U):
                step((NJ - 1) * U + i, r * NB + (NJ - 1) * U + i, r * NJ + (NJ - 1), i, U - 1 - i)

        def over_passes(eng, first, step):
            n = passes(eng)
            with eng.Fori(0, n) as r:
                first(r)
                each_block(eng, r, step)

        block = ctx.enter_context(nc.Block())

        @block.sync
        def _(sp):
            sp.dma_start(dst32, dst.rearrange("(b e) -> b e", b=NB)).then_inc(s_dst, 16)
            sp.wait_ge(s_pool, 1)
            sp.dma_start(xn[0:96, :, :], x[0:96 * S, :].rearrange("(p s) c -> p s c", s=S)).then_inc(s_in, 16)
            sp.dma_start(xn[96:97, :, :], x[96 * S:97 * S, :].rearrange("(p s) c -> p s c", s=S)).then_inc(s_in, 16)
            sp.dma_start(xn[97:98, 0:N - 97 * S, :], x[97 * S:N, :].rearrange("(p s) c -> p s c", p=1)).then_inc(s_in, 16)
            sp.dma_start(wtp[:], tp_T).then_inc(s_wts, 16)
            sp.dma_start(wtt[:], weight_T).then_inc(s_wts, 16)
            sp.dma_start(b0[:], bias0.rearrange("(p n) -> p n", p=1).broadcast_to([NP, C])).then_inc(s_wts, 16)
            for g in range(6):
                sp.dma_start(kf[g * C:(g + 1) * C, :], kern).then_inc(s_in, 16)
            for g in range(2):
                sp.dma_start(kf[2 * R + g:2 * R + g + 1, :], bias1.rearrange("(p n) -> p n", p=1)).then_inc(s_in, 16)
            sp.wait_ge(s_cast, 1)
            sp.dma_start(dst16_d, dst16).then_inc(s_d16, 16)
            sp.wait_ge(s_minmax, 1)
            sp.dma_start(w0_d.rearrange("k b -> b k"), w0s[:], allow_slow_non_contiguous=True).then_inc(s_w0, 16)
            sp.wait_ge(s_w0, 16)
            sp.dma_start(w0b[:].rearrange("p k b -> p (k b)"),
                         w0_d.rearrange("k b -> (k b)").rearrange("(o n) -> o n", o=1).broadcast_to([WIN, 2 * NB])
                         ).then_inc(s_wb, 16)
            sp.wait_ge(s_gp, 1)
            for l in range(2):
                sp.dma_start(xtab_d[l][NP * S:, :].rearrange("(p s) c -> p (s c)", s=16), zeros[0:WIN // 16, :]
                             ).then_inc(s_xtab, 16)
            sp.wait_ge(s_xpart, 1)
            sp.dma_start(xtab_d[0][0:NP * S, :].rearrange("(p s) c -> p (s c)", s=S),
                         xpart[:].rearrange("p s k c -> p (s k c)")).then_inc(s_xtab, 16)
            sp.wait_ge(s_d16, 16)
            sp.wait_ge(s_ready, 1)

            def load_dst(z, b, n, u, i):
                sp.wait_ge(z.woh_ready, slot_free(n))
                sp.sem_inc(s_sp_waits, 1)
                sp.dma_start(dstb[:, i, :], dst16_d[bass.ds(b, 1), :].broadcast_to([WIN, BE])
                             ).then_inc(z.dst_in[i], 16)

            def load_window(z, b, n, i):
                sp.wait_ge(z.gathered, slot_free(n))
                sp.sem_inc(s_sp_waits, 1)
                row = sp.value_load(wrow[z.l][0:1, bass.ds(b, 1)], min_val=0, max_val=NP * S)
                sp.dma_start(win[:, i, :], xtab_d[z.l][bass.ds(row, WIN), :]).then_inc(z.win_in[i], 16)

            def loads0(b, n, u, i):
                z = L[0]
                load_dst(z, b, n, u, i)
                sp.wait_ge(z.hi_ready, slot_free(n))
                sp.sem_inc(s_sp_waits, 1)
                sp.dma_start(srcr[:, i, :], src.rearrange("(b p t) -> b p t", b=NB, p=P)[bass.ds(b, 1), :, :]
                             .rearrange("o p t -> (o p) t")).then_inc(z.src_in[i], 16)
                sp.wait_ge(z.e_split, slot_free(n))
                sp.wait_ge(z.e_max, slot_free(n))
                sp.sem_inc(s_sp_waits, 1)
                sp.dma_start(efr[:, i, :], edge_T.rearrange("c e -> (c e)").rearrange("(b p n) -> b p n", b=NB, p=P)
                             [bass.ds(b, 1), :, :].rearrange("o p n -> (o p) n")).then_inc(z.ef_in[i], 16)

            def first0(r):
                sp.wait_ge(L[0].rows_ready, r * 2 + 2)
                sp.sem_inc(s_sp_waits, 1)
                for i in range(2):
                    loads0(i, r * NB + i, r * NJ, i)
                    if i == 0:
                        sp.wait_ge(s_xtab, 48)
                    load_window(L[0], i, r * NB + i, i)

            def step0(b, n, u, i, left):
                z = L[0]
                if left >= 2:
                    loads0(b + 2, n + 2, (u + 1 if i else u), (i + 2) % U)
                    load_window(z, b + 2, n + 2, (i + 2) % U)
                sp.wait_ge(z.mask_ready, block_done(n))
                sp.sem_inc(s_sp_waits, 1)
                sp.dma_start(nodes_d[bass.ds(b, 1), :, :].rearrange("o p n -> (o p) n"), nodes[:, i, :]
                             ).then_inc(z.nodes_out[i], 16)
                for k in range(NK):
                    sp.wait_ge(z.hoh_act, chunk_done(n * NK + k))
                    sp.sem_inc(s_sp_waits, 1)
                    sp.dma_start(hoh_d[bass.ds(b, 1), k, :, :].rearrange("o p n -> (o p) n"), hoh[:, k, 0, :]
                                 ).then_inc(z.kept_out[k], 16)

            for i in range(U):
                sp.sem_inc(L[0].nodes_out[i], 16)
            for k in range(NK):
                sp.sem_inc(L[0].kept_out[k], 16)
            over_passes(sp, first0, step0)
            cnt = passes(sp)
            for i in range(U):
                sp.wait_ge(L[0].nodes_out[i], cnt * (NJ * 16) + 16)
                sp.sem_inc(s_sp_waits, 1)
            for k in range(NK):
                sp.wait_ge(L[0].kept_out[k], cnt * (NB * 16) + 16)
                sp.sem_inc(s_sp_waits, 1)

            def loads1(b, n, u, i):
                load_dst(L[1], b, n, u, i)
                sp.wait_ge(L[1].b_ready, blocks_chunks_free(n))
                sp.sem_inc(s_sp_waits, 1)
                for g in range(2):
                    sp.dma_start(est[R * g:R * (g + 1), i, 0:BE], ef_d[:, bass.ds(b * BE, BE)]
                                 ).then_inc(L[1].edge_in[i], 16)

            def load_nodes(b, n, i):
                sp.wait_ge(L[1].v_ready, blocks_chunks_free(n))
                sp.wait_ge(L[1].hoh_act, blocks_chunks_free(n))
                sp.sem_inc(s_sp_waits, 1)
                sp.dma_start(nodes[:, i, :], nodes_d[bass.ds(b, 1), :, :].rearrange("o p n -> (o p) n")
                             ).then_inc(L[1].nodes_in[i], 16)

            def first1(r):
                sp.wait_ge(L[1].rows_ready, r * 2 + 2)
                sp.sem_inc(s_sp_waits, 1)
                for i in range(2):
                    load_window(L[1], i, r * NB + i, i)

            def step1(b, n, u, i, left):
                z = L[1]
                ahead = b + 2 if left >= 2 else 1 - left
                loads1(ahead, n + 2, (u + 1 if i else u), (i + 2) % U)
                if left >= 2:
                    load_window(z, b + 2, n + 2, (i + 2) % U)
                for k in range(NK):
                    sp.wait_ge(z.scattered, ring_free(n * NK + k))
                    sp.sem_inc(s_sp_waits, 1)
                    sp.dma_start(hoh[:, k, 0, :], hoh_d[bass.ds(b, 1), k, :, :].rearrange("o p n -> (o p) n")
                                 ).then_inc(z.kept_in[k], 16)
                load_nodes(ahead, n + 2, (i + 2) % U)

            sp.wait_ge(s_ef, 1)
            for i in range(2):
                loads1(i, i, 0, i)
                load_nodes(i, i, i)
            sp.wait_ge(s_xpart, 2)
            sp.dma_start(xtab_d[1][0:NP * S, :].rearrange("(p s) c -> p (s c)", s=S),
                         xpart[:].rearrange("p s k c -> p (s k c)")).then_inc(s_xtab, 16)
            sp.wait_ge(s_xtab, 64)
            over_passes(sp, first1, step1)
            cnt = passes(sp)
            for i in range(2):
                sp.wait_ge(L[1].dst_in[i], cnt * (NJ * 16) + 16)
                sp.sem_inc(s_sp_waits, 1)
                sp.wait_ge(L[1].edge_in[i], cnt * (NJ * 32) + 32)
                sp.sem_inc(s_sp_waits, 1)
                sp.wait_ge(L[1].nodes_in[i], cnt * (NJ * 16) + 16)
                sp.sem_inc(s_sp_waits, 1)
            sp.wait_ge(s_y, 1)
            sp.dma_start(out[0:96 * S, :].rearrange("(p s) c -> p s c", s=S), y[0:96, :, :]).then_inc(s_out, 16)
            sp.dma_start(out[96 * S:97 * S, :].rearrange("(p s) c -> p s c", s=S), y[96:97, :, :]).then_inc(s_out, 16)
            sp.dma_start(out[97 * S:N, :].rearrange("(p s) c -> p s c", p=1), y[97:98, 0:N - 97 * S, :]).then_inc(s_out, 16)
            sp.wait_ge(s_out, 48)

        @block.gpsimd
        def _(pool):
            for z in L:
                pool.sem_inc(z.e_split, U)
                pool.sem_inc(z.rows_ready, 2)
                pool.sem_inc(z.hoh_pool, U * len(POOL_ONE_HOTS))
                pool.sem_inc(z.half_ready, CR)
                pool.sem_inc(z.quart_ready, CR)
                pool.sem_inc(z.ml_ready, CR)
                if POOL_SUMS:
                    pool.sem_inc(z.eighth_ready, len(POOL_SUMS))
                    pool.sem_inc(z.msg_pool, len(POOL_SUMS))
            nc.gpsimd.memset(xn[:], 0.0)
            nc.gpsimd.memset(kf[:], 0.0).then_inc(s_pool, 1)
            nc.gpsimd.iota(pcol[:], [[0, 1]], base=0, channel_multiplier=1, allow_small_or_imprecise_dtypes=True)
            nc.gpsimd.iota(iota_hi[:], [[LO, HI]], base=0, channel_multiplier=0, allow_small_or_imprecise_dtypes=True)
            nc.gpsimd.iota(iota_lo[:].rearrange("p (g l) w -> p g l w", g=2), [[0, 2], [1, LO], [0, 2]], base=0, channel_multiplier=0)
            nc.gpsimd.memset(ident[:], 0.0)
            nc.gpsimd.memset(lo_of_p[:], 1.0)
            nc.gpsimd.memset(kw[:], 1.0)
            nc.gpsimd.memset(zeros[:], 0.0).then_inc(s_gp, 1)
            pool.wait_ge(s_gp, 1)
            nc.gpsimd.affine_select(out=ident[:], in_=ident[:], compare_op=ALU.not_equal, fill=1.0, base=0,
                                    pattern=[[-1, 128]], channel_multiplier=1)
            nc.gpsimd.affine_select(out=lo_of_p[:], in_=lo_of_p[:], compare_op=ALU.is_ge, fill=0.0, base=0,
                                    pattern=[[-C, LO]], channel_multiplier=1).then_inc(s_gp, 1)
            nc.gpsimd.affine_select(out=kw[:, 0:1], in_=kw[:, 0:1], compare_op=ALU.is_ge, fill=0.0, base=R - 1,
                                    pattern=[[0, 1]], channel_multiplier=-1).then_inc(s_gp, 1)
            pool.wait_ge(s_gp, 3)
            nc.gpsimd.affine_select(out=lo_of_p[:], in_=lo_of_p[:], compare_op=ALU.is_ge, fill=0.0, base=C - 1,
                                    pattern=[[C, LO]], channel_multiplier=-1)
            nc.gpsimd.affine_select(out=kw[:, 0:1], in_=kw[:, 0:1], compare_op=ALU.not_equal, fill=1.0, base=-2 * R,
                                    pattern=[[0, 1]], channel_multiplier=1).then_inc(s_pool, 1)
            pool.wait_ge(s_pool, 2)
            nc.gpsimd.memset(est[2 * R:2 * R + 2, :, :].rearrange("p u n -> p (u n)").bitcast(I32), 0x3F803F80
                             ).then_inc(s_gp, 1)
            pool.wait_ge(s_gp, 4)
            pool.wait_ge(s_mx, 1)
            nc.gpsimd.partition_all_reduce(mxa[:], mx[:], 128, ABSMAX).then_inc(s_mxa, 1)

            pool.wait_ge(s_ready, 1)

            def move(z, r):
                pool.wait_ge(z.win_in[U - 1], r * (NJ * 16) + NJ * 16)
                pool.sem_inc(s_pool_waits, 1)
                nc.gpsimd.tensor_scalar(wrowf[z.l][:], wrowf[z.l][:], float(WIN), float(NP * S), ALU.add, ALU.min
                                        ).then_inc(z.rows_ready, 1)
                pool.wait_ge(z.rows_ready, r * 2 + 3)
                pool.sem_inc(s_pool_waits, 1)
                nc.gpsimd.tensor_copy(wrow[z.l][:], wrowf[z.l][:]).then_inc(z.rows_ready, 1)
                pool.wait_ge(z.rows_ready, r * 2 + 4)
                pool.sem_inc(s_pool_waits, 1)

            def split_edges(z, b, n, u, i):
                pool.wait_ge(z.ef_in[i], u * 16 + 16)
                pool.sem_inc(s_pool_waits, 1)
                nc.gpsimd.tensor_copy(eparts[:, 0, :], efr[:, i, :]).then_inc(z.e_high, 1)
                pool.wait_ge(z.e_high, n + 1)
                pool.sem_inc(s_pool_waits, 1)
                nc.gpsimd.tensor_tensor(er1[:], efr[:, i, :], eparts[:, 0, :], ALU.subtract).then_inc(z.e_rest, 1)
                pool.wait_ge(z.e_rest, n + 1)
                pool.sem_inc(s_pool_waits, 1)
                nc.gpsimd.tensor_copy(eparts[:, 1, :], er1[:]).then_inc(z.e_mid, 1)
                pool.wait_ge(z.e_mid, n + 1)
                pool.sem_inc(s_pool_waits, 1)
                nc.gpsimd.tensor_tensor(eparts[:, 2, :], er1[:], eparts[:, 1, :], ALU.subtract).then_inc(z.e_split, 1)
                pool.wait_ge(z.e_split, block_done(n))
                pool.sem_inc(s_pool_waits, 1)
                nc.gpsimd.dma_start(
                    ef_d.rearrange("(k c) e -> k (c e)", k=3).rearrange("k (b p n) -> b p k n", b=NB, p=P)
                    [bass.ds(b, 1), :, :, :].rearrange("o p k n -> (o p) k n"), eparts[:]).then_inc(z.ef_out[i], 16)

            def one_hot(z, n, i, k):
                a, t = CHUNKS[k] - 1, START[k] + CHUNKS[k] - 1
                pool.wait_ge(z.hi_ready, block_done(n))
                pool.wait_ge(z.scattered, ring_free(n * NK + k))
                pool.sem_inc(s_pool_waits, 1)
                nc.gpsimd.tensor_scalar(hoh[:, k, a, :], iota_hi[:], hi8[:, i, t:t + 1], None, ALU.is_equal
                                        ).then_inc(z.hoh_pool, 1)

            def halves(q, k, c):
                z, m = L[1], CHUNKS[k]
                pool.wait_ge(z.prod_ready, chunk_done(q))
                pool.wait_ge(z.quart_ready, banks_free(q))
                pool.sem_inc(s_pool_waits, 1)
                nc.gpsimd.tensor_tensor(half[:, c, 0:m, :, :], prod[:, k, 0:m, :, 0:C // 2],
                                        prod[:, k, 0:m, :, C // 2:C], ALU.add).then_inc(z.half_ready, 1)

            def quarters(n, q, k, c):
                z, m = L[1], CHUNKS[k]
                pool.wait_ge(z.half_ready, chunk_done(q))
                if k in POOL_SUMS:
                    pool.wait_ge(z.eighth_ready, among_free(n, k, POOL_SUMS))
                else:
                    pool.wait_ge(z.msg_dve, among_free(n, k, DVE_SUMS))
                pool.sem_inc(s_pool_waits, 1)
                nc.gpsimd.tensor_tensor(quart[:, k, 0:m, :, :], half[:, c, 0:m, :, 0:C // 4],
                                        half[:, c, 0:m, :, C // 4:C // 2], ALU.add).then_inc(z.quart_ready, 1)

            def eighths(n, q, k):
                z, m = L[1], CHUNKS[k]
                pool.wait_ge(z.quart_ready, chunk_done(q))
                pool.wait_ge(z.msg_pool, among_done(n, k, POOL_SUMS) - 1)
                pool.sem_inc(s_pool_waits, 1)
                nc.gpsimd.tensor_tensor(eighth[:, 0:m, :, :], quart[:, k, 0:m, :, 0:2], quart[:, k, 0:m, :, 2:4],
                                        ALU.add).then_inc(z.eighth_ready, 1)

            def messages(n, q, k):
                z, m = L[1], CHUNKS[k]
                pool.wait_ge(z.eighth_ready, among_done(n, k, POOL_SUMS))
                pool.wait_ge(z.ml_ready, ring_free(q))
                pool.sem_inc(s_pool_waits, 1)
                nc.gpsimd.tensor_tensor(msg[:, k, 0:m, :], eighth[:, 0:m, :, 0], eighth[:, 0:m, :, 1],
                                        ALU.add).then_inc(z.msg_pool, 1)

            def lows(q, k, c):
                z = L[1]
                n = CHUNKS[k]
                pool.wait_ge(z.mh_ready, chunk_done(q))
                pool.wait_ge(z.v_ready, ring_free(q))
                pool.sem_inc(s_pool_waits, 1)
                nc.gpsimd.tensor_tensor(mpart[:, k, 0:n, 1, :], msg[:, k, 0:n, :], mpart[:, k, 0:n, 0, :],
                                        ALU.subtract).then_inc(z.ml_ready, 1)

            def layer(z):
                def step(b, n, u, i, left):
                    if not z.l:
                        split_edges(z, b, n, u, i)
                        for k in POOL_ONE_HOTS:
                            one_hot(z, n, i, k)
                    if z.l:
                        for k in range(NK):
                            q, c = n * NK + k, (i * NK + k) % 3
                            n3, k3 = n + (k + 3) // NK, (k + 3) % NK
                            if k + 3 < NK or left:
                                quarters(n3, q + 3, k3, c)
                            if k + 4 < NK or left:
                                halves(q + 4, (k + 4) % NK, (c + 1) % 3)
                            if k3 in POOL_SUMS and (k + 3 < NK or left):
                                eighths(n3, q + 3, k3)
                            if k + 2 < NK or left:
                                lows(q + 2, (k + 2) % NK, (c + 2) % 3)
                            if k3 in POOL_SUMS and (k + 3 < NK or left):
                                messages(n3, q + 3, k3)
                    else:
                        pool.wait_ge(z.ef_out[i], u * 16 + 16)
                        pool.sem_inc(s_pool_waits, 1)

                n = passes(pool)
                with pool.Fori(0, n) as r:
                    if z.l:
                        q = r * NB * NK
                        halves(q, 0, 0)
                        halves(q + 1, 1, 1)
                        for k in range(3):
                            if k:
                                halves(q + k + 1, k + 1, (k + 1) % 3)
                            quarters(r * NB, q + k, k, k)
                            if k in POOL_SUMS:
                                eighths(r * NB, q + k, k)
                                messages(r * NB, q + k, k)
                        lows(q, 0, 0)
                        lows(q + 1, 1, 1)
                    each_block(pool, r, step)
                    move(z, r)

            pool.wait_ge(s_wrep, 1)
            layer(L[0])
            pool.sem_inc(s_ef, 1)
            pool.wait_ge(s_em, 1)
            nc.gpsimd.partition_all_reduce(emx[:, 1:2], emx[:, 0:1], 128, ABSMAX).then_inc(s_ema, 1)
            layer(L[1])

        @block.scalar
        def _(act):
            for z in L:
                act.sem_inc(z.g_copied, U)
                act.sem_inc(z.hoh_act, CR)
                act.sem_inc(z.mh_ready, CR)
            act.wait_ge(s_dst, 16)
            nc.scalar.copy(dst16, dst32).then_inc(s_cast, 1)
            act.wait_ge(s_wrep, 1)
            nc.scalar.copy(wrep[:], ps[:, 2, 0:C * C]).then_inc(s_wrep, 1)
            act.wait_ge(s_ready, 1)

            def copy_gathered(z, n, i):
                act.wait_ge(z.gathered, block_done(n))
                if z.l == 0:
                    act.wait_ge(z.v_ready, blocks_chunks_free(n))
                    nc.scalar.copy(gparts[:, i, :, :].rearrange("p t c -> p (t c)"),
                                   ps[0:P, 1:3, :].rearrange("p a n -> p (a n)")[:, 0:T * 2 * C]).then_inc(z.g_copied, 1)
                else:
                    act.wait_ge(z.prod_ready, blocks_chunks_free(n))
                    nc.scalar.activation(gsum[:, i, :, :], ps[0:P, 1, 0:T * C].rearrange("p (t c) -> p t c", t=T),
                                         ACT.Copy, scale=mscf[0:P, 0:1]).then_inc(z.g_copied, 1)

            def distances(z, n, u, q, k, i, c):
                if k == 0:
                    if z.l:
                        act.wait_ge(z.nodes_in[i], u * 16 + 16)
                    else:
                        act.wait_ge(z.hi_ready, block_done(n))
                act.wait_ge(z.hoh_act, banks_free(q))
                for a in range(ACT_TILES[z.l][k]):
                    t = START[k] + KEPT[z.l] + a
                    ins = nc.scalar.activation(habs[:, c, a, :], iota_hi[:], ACT.Abs, bias=hi8[:, i, t:t + 1],
                                               scale=-1.0)
                ins.then_inc(z.abs_ready, 1)

            def one_hots(z, n, q, k, c):
                m = ACT_TILES[z.l][k]
                act.wait_ge(z.abs_ready, q + 1)
                act.wait_ge(z.scattered, ring_free(q))
                if not z.l:
                    act.wait_ge(z.kept_out[k], n * 16 + 16)
                nc.scalar.activation(hoh[:, k, KEPT[z.l]:KEPT[z.l] + m, :], habs[:, c, 0:m, :], ACT.Relu, bias=1.0, scale=-1.0
                                     ).then_inc(z.hoh_act, 1)

            def highs(n, q, k):
                z, m = L[1], CHUNKS[k]
                if k in POOL_SUMS:
                    act.wait_ge(z.msg_pool, among_done(n, k, POOL_SUMS))
                else:
                    act.wait_ge(z.msg_dve, among_done(n, k, DVE_SUMS))
                act.wait_ge(z.v_ready, ring_free(q))
                nc.scalar.copy(mpart[:, k, 0:m, 0, :], msg[:, k, 0:m, :]).then_inc(z.mh_ready, 1)

            def layer(z):
                if z.l:
                    act.wait_ge(s_msc, 1)

                def first(r):
                    copy_gathered(z, r * NB, 0)
                    for k in range(2):
                        distances(z, r * NB, r * NJ, r * NB * NK + k, k, 0, k)
                    one_hots(z, r * NB, r * NB * NK, 0, 0)
                    if z.l:
                        for k in range(2):
                            highs(r * NB, r * NB * NK + k, k)

                def step(b, n, u, i, left):
                    for k in range(NK):
                        q, c = n * NK + k, (i * NK + k) % 3
                        if k + 2 < NK:
                            distances(z, n, u, q + 2, k + 2, i, (c + 2) % 3)
                        elif left:
                            distances(z, n + 1, (u + 1 if i == U - 1 else u), q + 2, k + 2 - NK, (i + 1) % U,
                                      (c + 2) % 3)
                        if k + 1 < NK or left:
                            one_hots(z, n + (k + 1) // NK, q + 1, (k + 1) % NK, (c + 1) % 3)
                        if z.l and (k + 2 < NK or left):
                            highs(n + (k + 2) // NK, q + 2, (k + 2) % NK)
                        if k == max(GATHER[z.l]) + (z.l == 0) and left:
                            copy_gathered(z, n + 1, (i + 1) % U)

                over_passes(act, first, step)

            layer(L[0])
            act.wait_ge(L[0].acc_ready, 1)
            nc.scalar.activation(accs[:], acc, ACT.Copy, scale=invf[:, 0:1]).then_inc(s_accs, 1)
            act.wait_ge(s_var, 1)
            nc.scalar.sqrt(st[:, 2, :], st[:, 1, :]).then_inc(s_std, 1)
            layer(L[1])
            act.wait_ge(L[1].acc_ready, 1)
            nc.scalar.activation(accs[:], acc, ACT.Copy, scale=outs[:, 0:1]).then_inc(s_accs, 1)
            act.wait_ge(s_var, 2)
            nc.scalar.sqrt(st[:, 2, :], st[:, 1, :]).then_inc(s_std, 1)

        @block.vector
        def _(dve):
            for z in L:
                dve.sem_inc(z.woh_ready, U)
                dve.sem_inc(z.hi_ready, U)
                dve.sem_inc(z.mask_ready, U)
                dve.sem_inc(z.e_max, U)
                dve.sem_inc(z.v_ready, CR)
                dve.sem_inc(z.prod_ready, CR)
                dve.sem_inc(z.msg_dve, len(DVE_SUMS))
            chain = [0]

            def link(ins):
                chain[0] += 1
                ins.then_inc(s_dv, 1)
                dve.wait_ge(s_dv, chain[0])

            dve.wait_ge(s_dst, 16)
            nc.vector.tensor_reduce(w0s[:, 0:1], dst32, AX.X, ALU.min)
            nc.vector.tensor_reduce(w0s[:, 1:2], dst32, AX.X, ALU.max).then_inc(s_minmax, 1)
            nc.vector.memset(woh[:, :, BE:], 0.0)
            nc.vector.memset(emx[:], 1.0)
            link(nc.vector.memset(mx[:], 1e-20))
            dve.wait_ge(s_in, 11 * 16)
            nc.vector.tensor_reduce(mx[0:NP, 0:1], xn[:].rearrange("p s c -> p (s c)"), AX.X, ALU.max,
                                    apply_absolute_value=True)
            link(nc.vector.tensor_reduce(mx[0:2 * R + 2, 1:2], kf[:], AX.X, ALU.max, apply_absolute_value=True))
            nc.vector.tensor_scalar(mx[:], mx[:], 1e-20, None, ALU.max).then_inc(s_mx, 1)
            dve.wait_ge(s_wts, 48)
            nc.vector.tensor_copy(wtr, wtp[:].unsqueeze(2).broadcast_to([C, C, LO, C])).then_inc(s_wt, 1)
            dve.wait_ge(s_mxa, 1)
            link(nc.vector.tensor_single_scalar(mxe[:], mxa[:].bitcast(I32), EXP, ALU.bitwise_and))
            nc.vector.tensor_scalar(inv[:], mxe[:], -float(14 * ONE), None, ALU.add)
            link(nc.vector.tensor_scalar(scl[:], mxe[:], -1.0, float(TOP), ALU.mult, ALU.add))

            def split(values, scale):
                link(nc.vector.tensor_scalar(yd[:], values[:], scale, None, ALU.mult))
                link(nc.vector.tensor_copy(xpart[:, :, 0, :], yd[:]))
                nc.vector.tensor_tensor(xpart[:, :, 1, :], yd[:], xpart[:, :, 0, :], ALU.subtract
                                        ).then_inc(s_xpart, 1)

            split(xn, scf[0:NP, 0:1])
            dve.wait_ge(s_wb, 16)
            dve.wait_ge(s_pool, 2)
            for l in range(2):
                nc.vector.tensor_scalar(wnode[l][:], w0b[:, 0, :], pcol[:, 0:1], None, ALU.add)
                nc.vector.tensor_copy(wrowf[l][:], w0b[0:1, 0, :])
                nc.vector.tensor_copy(wrow[l][:], w0b[0:1, 0, :])
            link(nc.vector.tensor_tensor(span[:], w0b[:, 1, :], w0b[:, 0, :], ALU.subtract))
            link(nc.vector.tensor_reduce(spanmax[:], span[0:1, :], AX.X, ALU.max))
            link(nc.vector.tensor_copy(npass[:, 1:2], spanmax[:]))
            link(nc.vector.tensor_single_scalar(npass[:, 2:3], npass[:, 1:2], 7, ALU.logical_shift_right))
            nc.vector.tensor_scalar(npass[:, 0:1], npass[:, 2:3], 1.0, None, ALU.add).then_inc(s_ready, 1)
            dve.wait_ge(s_ready, 1)
            link(nc.vector.tensor_scalar(kf[:], kf[:], scf[0:2 * R + 2, 1:2], None, ALU.mult))
            link(nc.vector.tensor_copy(kh[:], kf[:]))
            link(nc.vector.tensor_tensor(kl[:], kf[:], kh[:], ALU.subtract))
            link(nc.vector.tensor_scalar(kw[:, 1:2], kw[:, 0:1], -1.0, 1.0, ALU.mult, ALU.add))
            link(nc.vector.tensor_scalar(kl[:], kl[:], kw[:, 1:2], None, ALU.mult))
            link(nc.vector.scalar_tensor_tensor(kst[:], kh[:], kw[:, 0:1], kl[:], ALU.mult, ALU.add))

            dve.wait_ge(s_wrep, 2)
            for lo in range(LO):
                ins = nc.vector.tensor_scalar(wblk[:, lo, :], wrep[:], lo_of_p[:, lo:lo + 1], None, ALU.mult)
            ins.then_inc(s_wblk, 1)

            def window_one_hot(z, b, n, u, i):
                dve.wait_ge(z.dst_in[i], u * 16 + 16)
                dve.wait_ge(z.gathered, slot_free(n))
                nc.vector.tensor_scalar(woh[:, i, 0:BE], dstb[:, i, :], wnode[z.l][:, bass.ds(b, 1)], None, ALU.is_equal
                                        ).then_inc(z.woh_ready, 1)

            def split_src(z, n, u, i):
                dve.wait_ge(z.src_in[i], u * 16 + 16)
                nc.vector.tensor_single_scalar(
                    lor[:, i, :, :], srcr[:, i, :].bitcast(I16)[:, 0:2 * T:2].unsqueeze(2).broadcast_to([P, T, 2]),
                    LO - 1, ALU.bitwise_and).then_inc(z.lo_ready, 1)

            def masks(z, n, u, i):
                dve.wait_ge(z.hoh_act, blocks_chunks_free(n))
                dve.wait_ge(z.hoh_pool, n * len(POOL_ONE_HOTS) + len(POOL_ONE_HOTS))
                dve.wait_ge(z.lo_ready, n + 1)
                dve.wait_ge(z.nodes_out[i], u * 16 + 16)
                nc.vector.tensor_tensor(hi8[:, i, :], srcr[:, i, :].bitcast(I16)[:, 0:2 * T:2], lor[:, i, :, 0],
                                        ALU.subtract).then_inc(z.hi_ready, 1)
                nc.vector.tensor_tensor(lomask[:, i, :, :, :],
                                        lor[:, i, :, :].unsqueeze(2).broadcast_to([P, T, 2 * LO, 2]),
                                        iota_lo[:].unsqueeze(1).broadcast_to([P, T, 2 * LO, 2]), ALU.is_equal
                                        ).then_inc(z.mask_ready, 1)

            def largest_edge(z, b, n, u, i):
                dve.wait_ge(z.ef_in[i], u * 16 + 16)
                nc.vector.tensor_reduce(em[:, bass.ds(b, 1)], efr[:, i, :], AX.X, ALU.max, apply_absolute_value=True
                                        ).then_inc(z.e_max, 1)

            def one_hots(z, q, k, i, c):
                dve.wait_ge(z.scattered, ring_free(q))
                for a in range(KEPT[z.l] + ACT_TILES[z.l][k], CHUNKS[k] - (not z.l and k in POOL_ONE_HOTS)):
                    t = START[k] + a
                    nc.vector.tensor_scalar(hoh[:, k, a, :], iota_hi[:], hi8[:, i, t:t + 1], None, ALU.is_equal)

            def spread(z, k, i, c, parts):
                t, n = START[k], CHUNKS[k]
                mask = (lomask[:, i, t:t + n, :, :].rearrange("p t (g l) w -> p (t g) l w", g=2).unsqueeze(3)
                        .broadcast_to([P, 2 * n, LO, C // 2, 2]))
                nc.vector.tensor_tensor(
                    vst[:, k, 0:n, :, :].rearrange("p t g (l c w) -> p (t g) l c w", l=LO, w=2),
                    parts.rearrange("p t (g c w) -> p (t g) c w", g=2, w=2).unsqueeze(2)
                    .broadcast_to([P, 2 * n, LO, C // 2, 2]), mask, ALU.mult).then_inc(z.v_ready, 1)

            def products(n, q, k, i, c):
                z = L[1]
                if k == 0:
                    dve.wait_ge(z.g_copied, block_done(n))
                dve.wait_ge(z.b_ready, chunk_done(q))
                dve.wait_ge(z.half_ready, ring_free(q))
                t, m = START[k], CHUNKS[k]
                nc.vector.tensor_tensor(
                    prod[:, k, 0:m, :, :],
                    ps[0:P, 2 + 2 * c:4 + 2 * c, :].rearrange("p a n -> p (a n)")[:, 0:m * C * C]
                    .rearrange("p (t i j) -> p t i j", t=m, i=C),
                    gsum[:, i, t:t + m, :].unsqueeze(2).broadcast_to([P, m, C, C]), ALU.mult).then_inc(z.prod_ready, 1)

            def messages(n, q, k):
                z, m = L[1], CHUNKS[k]
                dve.wait_ge(z.quart_ready, chunk_done(q))
                dve.wait_ge(z.ml_ready, ring_free(q))
                nc.vector.tensor_reduce(msg[:, k, 0:m, :], quart[:, k, 0:m, :, :], AX.X, ALU.add
                                        ).then_inc(z.msg_dve, 1)

            def layer(z):

                def step(b, n, u, i, left):
                    u1, i1 = (u + 1 if i == U - 1 else u), (i + 1) % U
                    for k in range(NK):
                        q, c = n * NK + k, (i * NK + k) % 3
                        if k == 5 and left >= 2:
                            window_one_hot(z, b + 2, n + 2, (u + 1 if i else u), (i + 2) % U)
                        if k == 3 and left and not z.l:
                            split_src(z, n + 1, u1, i1)
                        if k == 5 and not z.l:
                            largest_edge(z, b, n, u, i)
                        if k == 0:
                            if z.l:
                                dve.wait_ge(z.nodes_in[i], u * 16 + 16)
                            else:
                                dve.wait_ge(z.mask_ready, block_done(n))
                                dve.wait_ge(z.g_copied, block_done(n))
                        if z.l:
                            if k + 4 < NK:
                                products(n, q + 4, k + 4, i, (c + 1) % 3)
                            elif left:
                                products(n + 1, q + 4, k + 4 - NK, i1, (c + 1) % 3)
                            one_hots(z, q, k, i, c)
                            if (k + 2) % NK in DVE_SUMS and (k + 2 < NK or left):
                                messages(n + (k + 2) // NK, q + 2, (k + 2) % NK)
                            dve.wait_ge(z.ml_ready, chunk_done(q))
                            spread(z, k, i, c, mpart[:, k, 0:CHUNKS[k], :, :].rearrange("p t g c -> p t (g c)"))
                        else:
                            one_hots(z, q, k, i, c)
                            if k == 3 and left:
                                masks(z, n + 1, u1, i1)
                            t = START[k]
                            spread(z, k, i, c, gparts[:, i, t:t + CHUNKS[k], :])
                def first(r):
                    n = r * NB
                    window_one_hot(z, 0, n, r * NJ, 0)
                    window_one_hot(z, 1, n + 1, r * NJ, 1)
                    if not z.l:
                        split_src(z, n, r * NJ, 0)
                        masks(z, n, r * NJ, 0)
                    if z.l:
                        for k in range(4):
                            products(n, n * NK + k, k, 0, k % 3)
                        for k in range(2):
                            if k in DVE_SUMS:
                                messages(n, n * NK + k, k)

                cnt = passes(dve)
                with dve.Fori(0, cnt) as r:
                    first(r)
                    each_block(dve, r, step)
                    nc.vector.tensor_scalar(wnode[z.l][:], wnode[z.l][:], float(WIN), None, ALU.add).then_inc(z.moved, 1)
                    dve.wait_ge(z.moved, r + 1)

            def layer_norm(res, which):
                link(nc.vector.tensor_reduce(st[:, 0, :], y[:], AX.X, ALU.add))
                link(nc.vector.tensor_scalar(st[:, 0, :], st[:, 0, :], 1.0 / C, None, ALU.mult))
                link(nc.vector.tensor_tensor(yd[:], y[:], st[:, 0, :].unsqueeze(2).broadcast_to([NP, S, C]), ALU.subtract))
                link(nc.vector.tensor_tensor(yq[:], yd[:], yd[:], ALU.mult))
                link(nc.vector.tensor_reduce(st[:, 1, :], yq[:], AX.X, ALU.add))
                nc.vector.tensor_scalar(st[:, 1, :], st[:, 1, :], 1.0 / C, 1e-5, ALU.mult, ALU.add).then_inc(s_var, 1)
                dve.wait_ge(s_std, which)
                link(nc.vector.reciprocal(st[:, 3, :], st[:, 2, :]))
                return nc.vector.tensor_tensor(res[:], yd[:], st[:, 3, :].unsqueeze(2).broadcast_to([NP, S, C]), ALU.mult)

            dve.wait_ge(s_d16, 16)
            link(nc.vector.memset(est[0:2 * R, :, BE:], 0.0))
            layer(L[0])
            dve.wait_ge(L[0].e_max, U + 1)
            link(nc.vector.tensor_reduce(emx[0:P, 0:1], em[:], AX.X, ALU.max))
            nc.vector.tensor_scalar(emx[:, 0:1], emx[:, 0:1], 1.0, None, ALU.max).then_inc(s_em, 1)
            for a in range(A):
                dve.wait_ge(s_q, a + 1)
                bank = NODE_BANK[a % 2]
                nc.vector.tensor_tensor(
                    tq, ps[0:NP, bank:bank + 4, :].rearrange("p b n -> p (b n)").rearrange("p (l u o) -> p l u o", l=LO, u=C),
                    xn[:, a * LO:(a + 1) * LO, :].unsqueeze(3).broadcast_to([NP, LO, C, C]), ALU.mult).then_inc(s_qd, 1)
                dve.wait_ge(s_qd, a + 1)
                link(nc.vector.tensor_reduce(yq[:, a * LO:(a + 1) * LO, :], tq.rearrange("p l u o -> p l o u"), AX.X, ALU.add))
            link(nc.vector.tensor_tensor(y[:], xn[:], yq[:], ALU.add))
            link(nc.vector.tensor_tensor(y[:], y[:], b0[:].unsqueeze(1).broadcast_to([NP, S, C]), ALU.add))
            link(layer_norm(xn, 1))
            dve.wait_ge(s_xtab, 48)
            split(xn, X1S)
            dve.wait_ge(s_ema, 1)
            link(nc.vector.tensor_single_scalar(eme[:], emx[:, 1:2].bitcast(I32), EXP, ALU.bitwise_and))
            nc.vector.tensor_scalar(msc[:, 1:2], eme[:], float(MSGX * ONE), None, ALU.add)
            link(nc.vector.tensor_scalar(msc[:, 0:1], eme[:], -1.0, float((254 - MSGX) * ONE), ALU.mult, ALU.add))
            dve.sem_inc(s_msc, 1)
            link(nc.vector.tensor_tensor(outs[:], invf[:, 1:2], mscf[:, 1:2], ALU.mult))
            link(nc.vector.tensor_scalar(outs[:], outs[:], 1.0 / X1S, None, ALU.mult))
            layer(L[1])
            for a in range(A):
                dve.wait_ge(s_q, A + a + 1)
                link(nc.vector.tensor_tensor(y[:, a * LO:(a + 1) * LO, :], xn[:, a * LO:(a + 1) * LO, :],
                                             ps[0:NP, 2 + a, 0:128].rearrange("p (l c) -> p l c", l=LO), ALU.add))
            layer_norm(y, 2).then_inc(s_y, 1)

        @block.tensor
        def _(pe):
            for z in L:
                pe.sem_inc(z.gathered, U)
                pe.sem_inc(z.scattered, CR)
                pe.sem_inc(z.b_ready, CR)
            pe.wait_ge(s_wt, 1)
            for u in range(C):
                ins = nc.tensor.matmul(ps[:, 2, u * C:(u + 1) * C], wtr[:, u, :, :].rearrange("w l v -> w (l v)"),
                                       wtt[:], start=True, stop=True)
            ins.then_inc(s_wrep, 1)
            pe.wait_ge(s_ready, 1)

            def gather(z, n, u, i, tiles=range(T)):
                if tiles[0] == 0:
                    pe.wait_ge(z.woh_ready, block_done(n))
                    pe.wait_ge(z.win_in[i], u * 16 + 16)
                    pe.wait_ge(z.g_copied, n + U)
                for t in tiles:
                    edges = woh[:, i, t * P:t * P + PF]
                    if z.l == 0:
                        bank, at = (1, t) if t < G_SPLIT else (2, t - G_SPLIT)
                        ins = nc.tensor.matmul(ps[:, bank, at * 2 * C:(at + 1) * 2 * C], edges, win[:, i, :],
                                               start=True, stop=True)
                    else:
                        for g in range(2):
                            ins = nc.tensor.matmul(ps[:, 1, t * C:(t + 1) * C], edges, win[:, i, g * C:(g + 1) * C],
                                                   start=(g == 0), stop=(g == 1))
                if tiles[-1] == T - 1:
                    ins.then_inc(z.gathered, 1)

            def edge_matrices(z, n, u, q, k, i, c):
                if k == 0:
                    pe.wait_ge(z.edge_in[i], u * 32 + 32)
                pe.wait_ge(z.prod_ready, banks_free(q))
                for a in range(CHUNKS[k]):
                    t = START[k] + a
                    ins = nc.tensor.matmul(ps[:, 2 + 2 * c + a // 2, (a % 2) * C * C:(a % 2 + 1) * C * C],
                                           est[:, i, t * P:t * P + PF], kst[:], start=True, stop=True)
                ins.then_inc(z.b_ready, 1)

            def scatter(z, n, q, k):
                pe.wait_ge(z.v_ready, chunk_done(q))
                pe.wait_ge(z.hoh_act, chunk_done(q))
                if z.l:
                    pe.wait_ge(z.kept_in[k], n * 16 + 16)
                elif k in POOL_ONE_HOTS:
                    pe.wait_ge(z.hoh_pool, one_hot_done(n, k))
                for a in range(CHUNKS[k]):
                    for g in range(2):
                        ins = nc.tensor.matmul(acc, vst[:, k, a, g, :], hoh[:, k, a, :], start=False, stop=False,
                                               skip_group_check=True)
                ins.then_inc(z.scattered, 1)

            def layer(z):
                nc.tensor.matmul(acc, zeros[:, 0:128], zeros[:, 0:HI], start=True, stop=False, skip_group_check=True)

                def first(r):
                    gather(z, r * NB, r * NJ, 0)
                    if z.l:
                        for k in range(5):
                            edge_matrices(z, r * NB, r * NJ, r * NB * NK + k, k, 0, k % 3)

                def step(b, n, u, i, left):
                    u1 = u + 1 if i == U - 1 else u
                    for k in range(NK):
                        q, c = n * NK + k, (i * NK + k) % 3
                        if z.l:
                            if k + 5 < NK:
                                edge_matrices(z, n, u, q + 5, k + 5, i, (c + 2) % 3)
                            elif left:
                                edge_matrices(z, n + 1, u1, q + 5, k + 5 - NK, (i + 1) % U, (c + 2) % 3)
                        if k in GATHER[z.l] and left:
                            gather(z, n + 1, u1, (i + 1) % U, GATHER[z.l][k])
                        scatter(z, n, q, k)

                over_passes(pe, first, step)
                nc.tensor.matmul(acc, zeros[:, 0:128], zeros[:, 0:HI], start=False, stop=True, skip_group_check=True
                                 ).then_inc(z.acc_ready, 1)

            layer(L[0])
            pe.wait_ge(s_accs, 1)
            pe.wait_ge(s_wblk, 1)
            for a in range(A):
                if a >= 2:
                    pe.wait_ge(s_qd, a - 1)
                for h in range(4):
                    ins = nc.tensor.matmul(ps[0:NP, NODE_BANK[a % 2] + h, :], accs[:, a:HI:A],
                                           wblk.rearrange("p l n -> p (l n)")[:, h * 512:(h + 1) * 512],
                                           start=True, stop=True)
                ins.then_inc(s_q, 1)
            pe.wait_ge(s_qd, A)
            layer(L[1])
            pe.wait_ge(s_accs, 2)
            for a in range(A):
                nc.tensor.transpose(ps[0:NP, 2 + a, 0:128], accs[:, a:HI:A], ident[:]).then_inc(s_q, 1)


def kernel(x, src, dst, edge_attr_16, L0_gnn_W_tp, L0_gnn_weight, L0_gnn_bias, L1_gnn_kernel, L1_gnn_bias):
    import numpy as _np
    import concourse.bacc as _bacc
    from concourse import mybir as _mybir
    from concourse.bass_utils import run_bass_kernel_spmd as _run

    src_rows = _np.asarray(src).reshape(33, 25, 125).transpose(0, 2, 1).reshape(103125)
    laid = {
        "x": _np.asarray(x),
        "src": src_rows,
        "dst": _np.asarray(dst),
        "edge": _np.asarray(edge_attr_16).transpose(1, 0),
        "tp": _np.asarray(L0_gnn_W_tp).transpose(2, 0, 1),
        "weight": _np.asarray(L0_gnn_weight).transpose(1, 0),
        "bias0": _np.asarray(L0_gnn_bias),
        "kern": _np.asarray(L1_gnn_kernel),
        "bias1": _np.asarray(L1_gnn_bias),
    }
    nc = _bacc.Bacc("TRN2", target_bir_lowering=False, num_devices=1)
    arrays, args = {}, []
    for name, a in laid.items():
        a = _np.ascontiguousarray(a)
        arrays[f"in_{name}_dram"] = a
        args.append(nc.dram_tensor(f"in_{name}_dram", a.shape, _mybir.dt.from_np(a.dtype), kind="ExternalInput").ap())
    args.append(nc.dram_tensor("out_0_dram", (3125, 16), _mybir.dt.float32, kind="ExternalOutput").ap())
    bass_gnn_resnorm_two_layers(nc, *args)
    r = _run(nc, [arrays], core_ids=[0])
    return r.results[0]["out_0_dram"]
```
